# Optimizing a Trainium2 kernel written in Bass

```python
import numpy as np
import jax
import jax.numpy as jnp

def _softmax(x, axis=-1):
    return jax.nn.softmax(x, axis=axis)

def _gelu(x):
    return jax.nn.gelu(x, approximate=True)

def _silu(x):
    return jax.nn.silu(x)

def _sigmoid(x):
    return jax.nn.sigmoid(x)

def _layernorm(x, axis=-1, eps=1e-05):
    m = jnp.mean(x, axis=axis, keepdims=True)
    v = jnp.var(x, axis=axis, keepdims=True)
    return (x - m) / jnp.sqrt(v + eps)

def _scatter_add(tgt, idx, src, axis=0):
    return tgt.at[idx].add(src)

def _segment_sum(src, seg, n):
    return jax.ops.segment_sum(src, seg, n)
kernel_name = 'mk_adj_preln_d2_adj_r2_ffab6e'

def setup_inputs(seed: int=0):
    np.random.seed(seed)
    _w = jnp.asarray

    def _rec_inputs():
        import jax
        import jax.numpy as jnp
        _gk = jax.random.key(seed)
        x = -0.0002928 + 1 * jax.random.normal(jax.random.fold_in(_gk, 1), (8, 1024, 256), jnp.float32)
        _a = jax.random.bernoulli(jax.random.fold_in(_gk, 2), 0.00390625, (8, 1024, 1024))
        _a = jnp.logical_or(_a, jnp.swapaxes(_a, -1, -2))
        _a = jnp.logical_or(_a, jnp.eye(1024, dtype=bool))
        _af = _a.astype(jnp.float32)
        _af = _af * jax.random.uniform(jax.random.fold_in(_gk, 3), (8, 1024, 1024), jnp.float32, 0.05, 1)
        adj = _af
        return (x, adj)
    x, adj = _rec_inputs()

    def _L0_gnn_setup():
        import jax, jax.numpy as jnp
        import numpy as np
        B, N, DIN, DOUT, K = (4, 1024, 256, 256, 3)
        key = jax.random.key(seed)
        ks = jax.random.split(key, 8)
        X = jax.random.normal(ks[0], (B, N, DIN), dtype=jnp.float32)
        A = jax.random.uniform(ks[1], (B, N, N), dtype=jnp.float32)
        Wv = jax.random.normal(ks[2], (DIN, DOUT), dtype=jnp.float32) * 0.02
        bv = jax.random.normal(ks[3], (DOUT,), dtype=jnp.float32) * 0.02
        aw = jax.random.normal(ks[4], (2 * DOUT, 1), dtype=jnp.float32) * 0.05
        ab = jax.random.normal(ks[5], (1,), dtype=jnp.float32) * 0.05
        Wk = jax.random.normal(ks[6], (K, DIN, DOUT), dtype=jnp.float32) * 0.02
        bk = jax.random.normal(ks[7], (K, DOUT), dtype=jnp.float32) * 0.02
        return {'X': X, 'A': A, 'Wv': Wv, 'bv': bv, 'aw': aw, 'ab': ab, 'Wk': Wk, 'bk': bk}
    _L0_gnn_all = _L0_gnn_setup()
    _L0_gnn_in = {k: v for k, v in _L0_gnn_all.items() if k in ('Wv', 'bv', 'aw', 'ab', 'Wk', 'bk')}
    del _L0_gnn_all

    def _L1_gnn_setup():
        import jax, jax.numpy as jnp
        import numpy as np
        N = 4096
        F = 256
        C = 256
        key = jax.random.key(seed)
        k1, k2, k3 = jax.random.split(key, 3)
        X = jax.random.normal(k1, (1, N, F), dtype=jnp.float32)
        A = jax.random.uniform(k2, (1, N, N), dtype=jnp.float32)
        kernel = jax.random.normal(k3, (F, C), dtype=jnp.float32) * (1.0 / np.sqrt(F))
        bias = jnp.zeros((C,), dtype=jnp.float32)
        return {'X': X, 'A': A, 'kernel': kernel, 'bias': bias}
    _L1_gnn_all = _L1_gnn_setup()
    _L1_gnn_in = {k: v for k, v in _L1_gnn_all.items() if k in ('kernel', 'bias')}
    del _L1_gnn_all
    return {'x': x, 'adj': adj, 'L0_gnn_Wv': _L0_gnn_in['Wv'], 'L0_gnn_bv': _L0_gnn_in['bv'], 'L0_gnn_aw': _L0_gnn_in['aw'], 'L0_gnn_ab': _L0_gnn_in['ab'], 'L0_gnn_Wk': _L0_gnn_in['Wk'], 'L0_gnn_bk': _L0_gnn_in['bk'], 'L1_gnn_kernel': _L1_gnn_in['kernel'], 'L1_gnn_bias': _L1_gnn_in['bias']}

def reference(x, adj, L0_gnn_Wv, L0_gnn_bv, L0_gnn_aw, L0_gnn_ab, L0_gnn_Wk, L0_gnn_bk, L1_gnn_kernel, L1_gnn_bias):
    import jax
    import jax.numpy as jnp

    def _L0_gnn_ref(X, A, Wv, bv, aw, ab, Wk, bk):
        import jax, jax.numpy as jnp
        import numpy as np
        B, N, DIN, DOUT, K = (4, 1024, 256, 256, 3)
        d = Wv.shape[1]
        Xw = X @ Wv + bv
        sj = Xw @ aw[:d, 0]
        si = Xw @ aw[d:, 0]
        e = jax.nn.leaky_relu(sj[:, None, :] + si[:, :, None] + ab[0], negative_slope=0.2)
        alpha_matrix = A * jnp.exp(e)
        transition = alpha_matrix / (jnp.sum(alpha_matrix, axis=-1, keepdims=True) + 1e-12)
        H = jnp.zeros(X.shape[:-1] + (d,), dtype=X.dtype)
        Xk = X
        for k in range(Wk.shape[0]):
            H = H + Xk @ Wk[k] + bk[k]
            Xk = jnp.einsum('bij,bjd->bid', transition, Xk)
        return jax.nn.relu(H)

    def _L1_gnn_ref(X, A, kernel, bias):
        import jax, jax.numpy as jnp
        import numpy as np
        N = 4096
        F = 256
        C = 256
        Ah = A + jnp.eye(A.shape[-1], dtype=A.dtype)[None, :, :]
        dh = jax.lax.rsqrt(jnp.sum(Ah, axis=-1))
        An = dh[:, :, None] * Ah * dh[:, None, :]
        out = jnp.einsum('bnm,bmf,fc->bnc', An, X, kernel) + bias
        return jax.nn.relu(out)
    h = jnp.maximum(_layernorm(x, axis=-1), 0.0)
    x = x + _L0_gnn_ref(h, adj, L0_gnn_Wv, L0_gnn_bv, L0_gnn_aw, L0_gnn_ab, L0_gnn_Wk, L0_gnn_bk)
    h = jnp.maximum(_layernorm(x, axis=-1), 0.0)
    x = x + _L1_gnn_ref(h, adj, L1_gnn_kernel, L1_gnn_bias)
    return x

_drawn_inputs = setup_inputs


def setup_inputs(seed=0):
    import zlib

    import numpy as np

    out = dict(_drawn_inputs(seed))
    spreads = {'L1_gnn_bias': (0.0, 0.1)}
    factors = {'L0_gnn_Wv': 8.0, 'L0_gnn_bv': 27.023, 'L0_gnn_aw': 8.0}
    for name, (base, spread) in spreads.items():
        noise = np.random.default_rng([zlib.crc32(name.encode()), seed]).standard_normal(out[name].shape)
        drawn = base * np.exp(spread * noise) if base else spread * noise
        out[name] = jnp.asarray(drawn.astype(out[name].dtype))
    for name, factor in factors.items():
        out[name] = (out[name] * factor).astype(out[name].dtype)
    return out
```

```python
import numpy as np
import concourse.bass as bass
from concourse import mybir
from contextlib import ExitStack

F32 = mybir.dt.float32
F32R = mybir.dt.float32r
ALU = mybir.AluOpType
ACT = mybir.ActivationFunctionType



def gnn_two_layers(nc, x, adj, adj_t, wv_t, bv, aw, ab, wk, bk, w_l1, bias_l1, out):
    B, N, D = x.shape
    P = 128
    NT = N // P
    KD = D // P
    NG = NT // 2
    NU = NT
    HJ = NT // 2
    EARLY = 5
    TS, RS = 2, 4
    PHASES = 3 * NT
    EPS_LN, EPS_ROW, SLOPE = 1e-5, 1e-12, 0.2

    ctx = ExitStack()
    with ctx:
        def sb(name, shape, dt=F32):
            return ctx.enter_context(nc.sbuf_tensor(name, shape, dt))

        def pb(name, shape):
            return ctx.enter_context(nc.psum_tensor(name, shape, F32))

        def sem(name):
            return ctx.enter_context(nc.semaphore(name))

        t_hi = sb("t_hi", [P, NT, NT, P], F32R)
        t_lo = sb("t_lo", [P, NT, NT, P], F32R)
        tg_a = sb("tg_a", [P, TS, 2, HJ, P])
        tg_e = sb("tg_e", [P, TS, 2, HJ, P])
        a_raw = sb("a_raw", [P, RS, N])
        a_hi = sb("a_hi", [P, 2, NT, P], F32R)
        a_lo = sb("a_lo", [P, 2, NT, P], F32R)
        wa_hi = sb("wa_hi", [P, KD, 2 * D], F32R)
        wa_lo = sb("wa_lo", [P, KD, 2 * D], F32R)
        wb_hi = sb("wb_hi", [P, KD, D + 2], F32R)
        wb_lo = sb("wb_lo", [P, KD, D + 2], F32R)
        wl_hi = sb("wl_hi", [P, KD, D], F32R)
        wl_lo = sb("wl_lo", [P, KD, D], F32R)
        vi_hi = sb("vi_hi", [P, KD, P], F32R)
        vi_lo = sb("vi_lo", [P, KD, P], F32R)
        h0 = sb("h0", [P, NT, D])
        h1 = sb("h1", [P, 2, 2, D])
        x1 = sb("x1", [P, NT, D])
        ht_hi = sb("ht_hi", [P, 2, KD, 2 * P], F32R)
        ht_lo = sb("ht_lo", [P, 2, KD, 2 * P], F32R)
        p0 = sb("p0", [P, NT, D])
        p1 = sb("p1", [P, NT, D])
        g2_hi = sb("g2_hi", [P, NT, D + 2], F32R)
        g2_lo = sb("g2_lo", [P, NT, D], F32R)
        g1_hi = sb("g1_hi", [P, NT, D], F32R)
        g1_lo = sb("g1_lo", [P, NT, D], F32R)
        g1_tmp = sb("g1_tmp", [P, 2, D])
        si = sb("si", [P, N])
        sj = sb("sj", [P, NT])
        z_tmp = sb("z_tmp", [P, 2, D])
        o_tile = sb("o_tile", [P, 2, D])
        bk_sum = sb("bk_sum", [P, D])
        bias1 = sb("bias1", [P, D])
        ident = sb("ident", [P, P])
        st = sb("st", [P, NT, 6])
        mv0 = sb("mv0", [P, NT, 2])
        mv1 = sb("mv1", [P, NT, 2])
        ve0 = sb("ve0", [P, NT])
        ve1 = sb("ve1", [P, NT])
        rstd0 = sb("rstd0", [P, NT])
        rstd1 = sb("rstd1", [P, NT])
        row_a = sb("row_a", [P, NT])
        row_a1 = sb("row_a1", [P, NT])
        dh = sb("dh", [P, NT])
        mhalf = sb("mhalf", [P, NT])
        row_t = sb("row_t", [P, NT])
        rinv = sb("rinv", [P, NT])
        aw_s = sb("aw_s", [P, 2 * KD])
        bv_s = sb("bv_s", [P, KD])
        ab_s = sb("ab_s", [P, 1])
        bv_r = sb("bv_r", [P, KD, P])
        v_s = sb("v_s", [P, KD + 1, 2])
        cst = sb("cst", [P, 2])

        wk_raw = x1[:, :, :].rearrange("p (a k) n -> p a k n", k=KD)
        wvt_raw = p1[:, 0:KD, :]
        bk_raw = p0[:, 0:3, :]

        tp = pb("tp", [P, 2, KD, 2 * P])
        da = pb("da", [P, 2, 2 * D])
        db = pb("db", [P, 512])
        ps = pb("ps", [P, 512])
        acc = pb("acc", [P, 2, 512])

        loaded_c = sem("loaded_c")
        setup = sem("setup")
        ident_zero = sem("ident_zero")
        ident_ready = sem("ident_ready")
        v_ready = sem("v_ready")
        weights_ready = sem("weights_ready")
        h0_loaded = sem("h0_loaded")
        x1_loaded = sem("x1_loaded")
        tg_loaded = [sem(f"tg_loaded{s}") for s in range(TS)]
        raw_loaded = [sem(f"raw_loaded{s}") for s in range(RS)]
        stored = [sem(f"stored{s}") for s in range(2)]
        tp0_full, tp1_full = sem("tp0_full"), sem("tp1_full")
        si_full = sem("si_full")
        da_full, db_full, l1_full = sem("da_full"), sem("db_full"), sem("l1_full")
        acc_full = sem("acc_full")
        ht0_hi_done, ht1_hi_done = sem("ht0_hi_done"), sem("ht1_hi_done")
        ht0_ready, ht1_ready = sem("ht0_ready"), sem("ht1_ready")
        si_ready = sem("si_ready")
        g2_hi_done, g2_ready = sem("g2_hi_done"), sem("g2_ready")
        p0_ready = sem("p0_ready")
        score_done, leaky_done, e_ready = sem("score_done"), sem("leaky_done"), sem("e_ready")
        prod_ready = sem("prod_ready")
        t_hi_done, t_ready = sem("t_hi_done"), sem("t_ready")
        row_t_done, rinv_done = sem("row_t_done"), sem("rinv_done")
        g1_tmp_ready, g1_hi_done, g1_ready = sem("g1_tmp_ready"), sem("g1_hi_done"), sem("g1_ready")
        rows_done, rows1_done, dh_ready = sem("rows_done"), sem("rows1_done"), sem("dh_ready")
        stats0, mean0, ve0_ready, rstd0_ready = (sem(n) for n in ("stats0", "mean0", "ve0_ready", "rstd0_ready"))
        stats1, mean1, ve1_ready, rstd1_ready = (sem(n) for n in ("stats1", "mean1", "ve1_ready", "rstd1_ready"))
        stats_seen = sem("stats_seen")
        h0_ready, h1_ready = sem("h0_ready"), sem("h1_ready")
        v_tmp_done, x1_ready = sem("v_tmp_done"), sem("x1_ready")
        y_hi_done, y_ready = sem("y_hi_done"), sem("y_ready")
        diag_done, a_hi_done, a_ready = sem("diag_done"), sem("a_hi_done"), sem("a_ready")
        z_tmp_done, o_ready = sem("z_tmp_done"), sem("o_ready")

        x_v = x.rearrange("b (t p) d -> b p t d", p=P)
        out_v = out.rearrange("b (t p) d -> b p t d", p=P)
        adj_v = adj.rearrange("b (t p) j -> b p t j", p=P)

        def chunk(src, b, i):
            return src[b, i // 2, :, :, i % 2].rearrange("h p c -> p h c")

        def t_view(t, u):
            cp, jh = u // 2, u % 2
            return t[:, 2 * cp:2 * cp + 2, jh * HJ:(jh + 1) * HJ, :]

        def load_t_unit(eng, b, u):
            eng.dma_start(tg_a[:, u % TS].rearrange("p s q i -> p (s q i)"),
                          adj_t[b, u // 2, u % 2].rearrange("p s c -> p (s c)")).then_inc(tg_loaded[u % TS], 16)

        def next_unit(b, u, last):
            if u + TS < NU:
                return b, u + TS
            return None if last else (b + 1, u + TS - NU)

        block = ctx.enter_context(nc.Block())

        @block.sync
        def _(sp):
            sp.dma_start(h0[:, :, :], x_v[0]).then_inc(h0_loaded, 16)
            sp.dma_start(wk_raw[:, 0:3], wk.rearrange("a (k p) n -> p a k n", p=P)).then_inc(loaded_c, 16)
            sp.dma_start(wk_raw[:, 3], w_l1.rearrange("(k p) n -> p k n", p=P)).then_inc(loaded_c, 16)
            sp.dma_start(wvt_raw, wv_t.rearrange("(k p) n -> p k n", p=P)).then_inc(loaded_c, 16)
            sp.dma_start(bk_raw, bk.rearrange("(o a) n -> o a n", o=1).to_broadcast([P, 3, D])).then_inc(loaded_c, 16)
            sp.dma_start(bias1[:, :], bias_l1.rearrange("(o n) -> o n", o=1).to_broadcast([P, D])).then_inc(loaded_c, 16)
            with nc.allow_non_contiguous_dma(reason="three short vectors"):
                sp.dma_start(aw_s[:, :], aw.rearrange("(c p) o -> p (c o)", p=P)).then_inc(loaded_c, 16)
                sp.dma_start(bv_s[:, :], bv.rearrange("(c p) -> p c", p=P)).then_inc(loaded_c, 16)
                sp.dma_start(ab_s[:, :], ab.rearrange("(o n) -> o n", o=1).to_broadcast([P, 1])).then_inc(loaded_c, 16)
            sp.wait_ge(weights_ready, 1)
            sp.dma_start(x1[:, :, :], x_v[0]).then_inc(x1_loaded, 16)

            def rows(b):
                for t in range(NT):
                    if t < RS:
                        sp.wait_ge(a_ready, b * NT + t - RS + NT)
                    else:
                        sp.wait_ge(rows_done, b * NT + t - RS + 1)
                    sp.dma_start(a_raw[:, t % RS, :], adj_v[b, :, t]).then_inc(raw_loaded[t % RS], 16)

            def stores(b, i):
                sp.wait_ge(o_ready, b * NT + i + 1)
                sp.dma_start(out_v[b, :, i], o_tile[:, i % 2, :]).then_inc(stored[i % 2], 16)

            def batch(b, last):
                if not last:
                    sp.wait_ge(tp0_full, b * NG + NG)
                    sp.dma_start(h0[:, :, :], x_v[b + 1]).then_inc(h0_loaded, 16)
                rows(b)
                chunks_and_stores(b)
                if not last:
                    sp.dma_start(x1[:, :, :], x_v[b + 1]).then_inc(x1_loaded, 16)

            def chunks_and_stores(b):
                for i in range(NT):
                    if i < RS:
                        sp.wait_ge(rows_done, b * NT + NT - RS + i + 1)
                    else:
                        sp.wait_ge(a_ready, b * NT + i - RS + 1 + NT)
                    sp.dma_start(a_raw[:, i % RS, :].rearrange("p (h c) -> p h c", h=2),
                                 chunk(adj_t, b, i)).then_inc(raw_loaded[i % RS], 16)
                    if i >= RS:
                        stores(b, i - RS)
                for i in range(NT - RS, NT):
                    stores(b, i)

            with nc.sync.Fori(0, B - 1) as b:
                batch(b, False)
            batch(B - 1, True)
            for s in range(2):
                sp.wait_ge(stored[s], 16 * (B * NT // 2 + 1))

        @block.gpsimd
        def _(pool):
            pool.sem_inc(a_ready, NT)
            nc.gpsimd.memset(mhalf[:, :], -0.5)
            nc.gpsimd.memset(ident[:, :], 0.0).then_inc(ident_zero, 1)
            pool.wait_ge(ident_zero, 1)
            nc.gpsimd.affine_select(out=ident[:, :], in_=ident[:, :], compare_op=ALU.not_equal, fill=1.0,
                                    base=0, pattern=[[-1, P]], channel_multiplier=1).then_inc(ident_ready, 1)

            def power(dst, src, ready, done, b):
                pool.wait_ge(ready, b + 1)
                nc.gpsimd.tensor_tensor(dst[:, :], src[:, :], mhalf[:, :], ALU.pow).then_inc(done, 1)

            def batch(b, last):
                for i in range(NT):
                    pool.wait_ge(g1_hi_done, b * NT + i + 1)
                    nc.gpsimd.tensor_tensor(g1_lo[:, i, :], g1_tmp[:, i % 2, :], g1_hi[:, i, :].bitcast(F32),
                                            ALU.subtract).then_inc(g1_ready, 1)
                if not last:
                    power(rstd0, ve0, ve0_ready, rstd0_ready, b + 1)
                power(dh, row_a1, rows1_done, dh_ready, b)
                power(rstd1, ve1, ve1_ready, rstd1_ready, b)
                for i in range(NT):
                    pool.wait_ge(a_hi_done, b * NT + i + 1)
                    nc.gpsimd.tensor_tensor(a_lo[:, i % 2].rearrange("p q i -> p (q i)"), a_raw[:, i % RS, :],
                                            a_hi[:, i % 2].rearrange("p q i -> p (q i)").bitcast(F32),
                                            ALU.subtract).then_inc(a_ready, 1)

            power(rstd0, ve0, ve0_ready, rstd0_ready, 0)
            with nc.gpsimd.Fori(0, B - 1) as b:
                batch(b, False)
            batch(B - 1, True)

        @block.scalar
        def _(act):
            load_t_unit(act, 0, 0)
            load_t_unit(act, 0, 1)

            def transposed_hi(g, full, b, done):
                act.wait_ge(full, b * NG + g + 1)
                nc.scalar.activation(ht_hi[:, g % 2], tp[:, g % 2], ACT.Relu).then_inc(done, 1)

            def dense0(b, t):
                act.wait_ge(da_full, b * NT + t + 1)
                nc.scalar.copy(p1[:, t, :], da[:, t % 2, 0:D])
                nc.scalar.copy(g2_hi[:, t, 0:D], da[:, t % 2, D:2 * D]).then_inc(g2_hi_done, 1)

            def si_copy(b, g):
                act.wait_ge(si_full, b * NG + g + 1)
                nc.scalar.copy(si[:, g * 2 * P:(g + 1) * 2 * P], ps[:, 0:2 * P]).then_inc(si_ready, 1)

            def exps(b, u):
                cp, jh, s = u // 2, u % 2, u % TS
                act.wait_ge(t_ready, b * NU + u)
                for q in range(HJ):
                    jt = jh * HJ + q
                    ins = nc.scalar.activation(tg_e[:, s, :, q, :],
                                               si[:, cp * 2 * P:(cp + 1) * 2 * P].rearrange("p (s i) -> p s i", s=2),
                                               ACT.Identity, bias=sj[:, jt:jt + 1])
                ins.then_inc(score_done, 1)
                act.wait_ge(leaky_done, b * NU + u + 1)
                nc.scalar.activation(tg_e[:, s], tg_e[:, s], ACT.Exp).then_inc(e_ready, 1)

            def t_round(b, u, last):
                act.wait_ge(prod_ready, b * NU + u + 1)
                nc.scalar.copy(t_view(t_hi, u), tg_e[:, u % TS]).then_inc(t_hi_done, 1)
                nxt = next_unit(b, u, last)
                if nxt is not None:
                    load_t_unit(act, *nxt)

            def units(b, lo, hi, last):
                for u in range(lo, hi):
                    exps(b, u)
                    t_round(b, u, last)

            def layer0_dense(b):
                transposed_hi(0, tp0_full, b, ht0_hi_done)
                for g in range(NG):
                    if g + 1 < NG:
                        transposed_hi(g + 1, tp0_full, b, ht0_hi_done)
                    si_copy(b, g)
                    dense0(b, 2 * g)
                    dense0(b, 2 * g + 1)

            def batch(b, last):
                for i in range(NT):
                    if i < NU - EARLY:
                        exps(b, EARLY + i)
                        t_round(b, EARLY + i, last)
                    act.wait_ge(g1_tmp_ready, b * NT + i + 1)
                    nc.scalar.copy(g1_hi[:, i, :], g1_tmp[:, i % 2, :]).then_inc(g1_hi_done, 1)
                for t in range(NT):
                    act.wait_ge(raw_loaded[t % RS], 16 * (b * 2 * NT // RS + t // RS + 1))
                    nc.scalar.activation(a_raw[:, t % RS, :], a_raw[:, t % RS, :], ACT.Copy,
                                         accum_out=row_a[:, t:t + 1]).then_inc(rows_done, 1)
                if not last:
                    layer0_dense(b + 1)
                act.wait_ge(dh_ready, b + 1)

                def l1_scaled(t):
                    act.wait_ge(l1_full, b * NT + t + 1)
                    nc.scalar.activation(g1_hi[:, t, :], da[:, t % 2, 0:D], ACT.Copy,
                                         scale=dh[:, t:t + 1]).then_inc(y_hi_done, 1)

                def a_round(i):
                    act.wait_ge(diag_done, b * NT + i + 1)
                    if i >= 2:
                        act.wait_ge(acc_full, b * PHASES + 2 * NT + i - 1)
                    nc.scalar.copy(a_hi[:, i % 2].rearrange("p q i -> p (q i)"),
                                   a_raw[:, i % RS, :]).then_inc(a_hi_done, 1)

                transposed_hi(0, tp1_full, b, ht1_hi_done)
                for g in range(NG):
                    if g + 1 < NG:
                        transposed_hi(g + 1, tp1_full, b, ht1_hi_done)
                    if g in (1, 2):
                        a_round(g - 1)
                    l1_scaled(2 * g)
                    l1_scaled(2 * g + 1)
                for i in range(NT):
                    if i + 2 < NT:
                        a_round(i + 2)
                    if not last and i < EARLY:
                        exps(b + 1, i)
                        t_round(b + 1, i, last)

            layer0_dense(0)
            units(0, 0, EARLY, False)
            with nc.scalar.Fori(0, B - 1) as b:
                batch(b, False)
            batch(B - 1, True)

        @block.vector
        def _(dve):
            dve.sem_inc(z_tmp_done, 2)
            for s in range(2):
                dve.sem_inc(stored[s], 16)
            steps = [0]

            def then(ins):
                steps[0] += 1
                ins.then_inc(setup, 1)
                dve.wait_ge(setup, steps[0])

            dve.wait_ge(loaded_c, 16 * 8)
            nc.vector.memset(g2_hi[:, :, D:D + 2].bitcast(F32), 1.0)
            nc.vector.memset(wb_hi[:, :, D + 1:D + 2].bitcast(F32), 0.0)
            nc.vector.memset(wb_lo[:, :, D + 1:D + 2].bitcast(F32), 0.0)
            nc.vector.tensor_tensor(bk_sum[:, :], bk_raw[:, 0, :], bk_raw[:, 1, :], ALU.add)
            for k in range(KD):
                nc.vector.tensor_copy(bv_r[:, k, :], bv_s[:, k:k + 1].to_broadcast([P, P]))
            for a in range(2):
                nc.vector.tensor_copy(wa_hi[:, :, a * D:(a + 1) * D], wk_raw[:, a + 1])
            nc.vector.tensor_copy(wb_hi[:, :, 0:D], wk_raw[:, 0])
            then(nc.vector.tensor_copy(wl_hi[:, :, :], wk_raw[:, 3]))
            nc.vector.tensor_tensor(bk_sum[:, :], bk_sum[:, :], bk_raw[:, 2, :], ALU.add)
            for a in range(2):
                nc.vector.tensor_tensor(wa_lo[:, :, a * D:(a + 1) * D], wk_raw[:, a + 1],
                                        wa_hi[:, :, a * D:(a + 1) * D].bitcast(F32), ALU.subtract)
            nc.vector.tensor_tensor(wb_lo[:, :, 0:D], wk_raw[:, 0], wb_hi[:, :, 0:D].bitcast(F32), ALU.subtract)
            nc.vector.tensor_tensor(wl_lo[:, :, :], wk_raw[:, 3], wl_hi[:, :, :].bitcast(F32),
                                    ALU.subtract).then_inc(weights_ready, 1)
            dve.wait_ge(v_ready, 1)
            then(nc.vector.tensor_copy(v_s[:, :, :], db[:, 0:2 * (KD + 1)].rearrange("p (k c) -> p k c", c=2)))
            nc.vector.tensor_tensor(cst[:, 0:1], v_s[:, KD, 0:1], v_s[:, KD, 1:2], ALU.add)
            nc.vector.tensor_copy(wb_hi[:, :, D:D + 1], v_s[:, 0:KD, 0:1])
            for k in range(KD):
                ins = nc.vector.tensor_copy(vi_hi[:, k, :], v_s[:, k, 1:2].to_broadcast([P, P]))
            then(ins)
            nc.vector.tensor_tensor(cst[:, 1:2], cst[:, 0:1], ab_s[:, :], ALU.add)
            nc.vector.tensor_tensor(wb_lo[:, :, D:D + 1], v_s[:, 0:KD, 0:1], wb_hi[:, :, D:D + 1].bitcast(F32),
                                    ALU.subtract)
            for k in range(KD):
                ins = nc.vector.tensor_tensor(vi_lo[:, k, :], v_s[:, k, 1:2].to_broadcast([P, P]),
                                              vi_hi[:, k, :].bitcast(F32), ALU.subtract)
            ins.then_inc(weights_ready, 1)

            def moments(b, mv, ve, stats, mean, ve_ready):
                dve.wait_ge(stats, b + 1)
                dve.sem_inc(stats_seen, 1)
                for t in range(NT):
                    ins = nc.vector.bn_aggr(mv[:, t, :], st[:, t, :])
                ins.then_inc(mean, 1)
                dve.wait_ge(mean, b + 1)
                nc.vector.tensor_scalar_add(ve[:, :], mv[:, :, 1], EPS_LN).then_inc(ve_ready, 1)

            def stats_of(t, src, stats):
                ins = nc.vector.bn_stats(st[:, t, :], src[:, t, :])
                if t == NT - 1:
                    ins.then_inc(stats, 1)

            def norm(t, dst, src, mv, rstd, ready):
                nc.vector.tensor_scalar(dst, src[:, t, :], mv[:, t, 0:1], rstd[:, t:t + 1],
                                        ALU.subtract, ALU.mult).then_inc(ready, 1)

            def norm1(g):
                for s in range(2):
                    norm(2 * g + s, h1[:, g % 2, s, :], x1, mv1, rstd1, h1_ready)

            def transposed_lo(g, hi_done, b, ready):
                dve.wait_ge(hi_done, b * NG + g + 1)
                nc.vector.scalar_tensor_tensor(out=ht_lo[:, g % 2], in0=tp[:, g % 2], scalar=0.0,
                                               in1=ht_hi[:, g % 2].bitcast(F32),
                                               op0=ALU.max, op1=ALU.subtract).then_inc(ready, 1)

            def dense0(b, t):
                dve.wait_ge(g2_hi_done, b * NT + t + 1)
                nc.vector.tensor_tensor(g2_lo[:, t, :], da[:, t % 2, D:2 * D], g2_hi[:, t, 0:D].bitcast(F32),
                                        ALU.subtract).then_inc(g2_ready, 1)
                dve.wait_ge(db_full, b * NT + t + 1)
                nc.vector.tensor_tensor(p0[:, t, :], db[:, 0:D], bk_sum[:, :], ALU.add)
                nc.vector.tensor_tensor(sj[:, t:t + 1], db[:, D:D + 1], cst[:, 1:2], ALU.add).then_inc(p0_ready, 1)

            def layer0_dense(b, between=lambda g: None):
                transposed_lo(0, ht0_hi_done, b, ht0_ready)
                for g in range(NG):
                    if g + 1 < NG:
                        transposed_lo(g + 1, ht0_hi_done, b, ht0_ready)
                    dense0(b, 2 * g)
                    dense0(b, 2 * g + 1)
                    between(g)

            def t_unit(b, u):
                s = u % TS
                dve.wait_ge(score_done, b * NU + u + 1)
                nc.vector.scalar_tensor_tensor(out=tg_e[:, s], in0=tg_e[:, s], scalar=SLOPE, in1=tg_e[:, s],
                                               op0=ALU.mult, op1=ALU.max).then_inc(leaky_done, 1)
                dve.wait_ge(e_ready, b * NU + u + 1)
                dve.wait_ge(tg_loaded[s], 16 * (b * NU // TS + u // TS + 1))
                nc.vector.tensor_tensor(tg_e[:, s], tg_a[:, s], tg_e[:, s], ALU.mult).then_inc(prod_ready, 1)
                dve.wait_ge(t_hi_done, b * NU + u + 1)
                nc.vector.tensor_tensor(t_view(t_lo, u), tg_e[:, s], t_view(t_hi, u).bitcast(F32),
                                        ALU.subtract).then_inc(t_ready, 1)

            def batch(b, last):
                if not last:
                    dve.wait_ge(h0_loaded, 16 * (b + 2))
                for i in range(NT):
                    if i < NU - EARLY:
                        t_unit(b, EARLY + i)
                    s = i % 2
                    dve.wait_ge(acc_full, b * PHASES + i + 1)
                    nc.vector.tensor_scalar_add(row_t[:, i:i + 1], acc[:, s, D:D + 1], EPS_ROW).then_inc(row_t_done, 1)
                    if not last:
                        stats_of(i, h0, stats0)
                    dve.wait_ge(row_t_done, b * NT + i + 1)
                    nc.vector.reciprocal(rinv[:, i:i + 1], row_t[:, i:i + 1]).then_inc(rinv_done, 1)
                    dve.wait_ge(rinv_done, b * NT + i + 1)
                    if i >= 2:
                        dve.wait_ge(g1_ready, b * NT + i - 1)
                    nc.vector.scalar_tensor_tensor(out=g1_tmp[:, s, :], in0=acc[:, s, 0:D], scalar=rinv[:, i:i + 1],
                                                   in1=p1[:, i, :], op0=ALU.mult, op1=ALU.add)\
                        .then_inc(g1_tmp_ready, 1)
                if not last:
                    moments(b + 1, mv0, ve0, stats0, mean0, ve0_ready)
                dve.wait_ge(x1_loaded, 16 * (b + 1))
                for i in range(NT):
                    s = i % 2
                    dve.wait_ge(acc_full, b * PHASES + NT + i + 1)
                    nc.vector.scalar_tensor_tensor(out=p0[:, i, :], in0=acc[:, s, 0:D], scalar=rinv[:, i:i + 1],
                                                   in1=p0[:, i, :], op0=ALU.mult, op1=ALU.add).then_inc(v_tmp_done, 1)
                    if not last:
                        if i == 0:
                            dve.wait_ge(rstd0_ready, b + 2)
                        norm(i, h0[:, i, :], h0, mv0, rstd0, h0_ready)
                    dve.wait_ge(v_tmp_done, b * NT + i + 1)
                    nc.vector.scalar_tensor_tensor(out=x1[:, i, :], in0=p0[:, i, :], scalar=0.0, in1=x1[:, i, :],
                                                   op0=ALU.max, op1=ALU.add).then_inc(x1_ready, 1)
                    dve.wait_ge(x1_ready, b * NT + i + 1)
                    stats_of(i, x1, stats1)
                dve.wait_ge(rows_done, b * NT + NT)
                nc.vector.tensor_scalar_add(row_a1[:, :], row_a[:, :], 1.0).then_inc(rows1_done, 1)
                moments(b, mv1, ve1, stats1, mean1, ve1_ready)

                def between(g):
                    if g in (1, 2):
                        if g == 1:
                            dve.wait_ge(rstd1_ready, b + 1)
                        norm1(g - 1)

                if not last:
                    layer0_dense(b + 1, between)
                else:
                    between(1)
                    between(2)

                def diag(i):
                    dve.wait_ge(raw_loaded[i % RS], 16 * (b * 2 * NT // RS + NT // RS + i // RS + 1))
                    blk = a_raw[:, i % RS, i * P:(i + 1) * P]
                    nc.vector.tensor_tensor(blk, blk, ident[:, :], ALU.add).then_inc(diag_done, 1)

                def l1_low(t):
                    dve.wait_ge(y_hi_done, b * NT + t + 1)
                    nc.vector.scalar_tensor_tensor(out=g1_lo[:, t, :], in0=da[:, t % 2, 0:D], scalar=dh[:, t:t + 1],
                                                   in1=g1_hi[:, t, :].bitcast(F32), op0=ALU.mult, op1=ALU.subtract)\
                        .then_inc(y_ready, 1)

                diag(0)
                diag(1)
                transposed_lo(0, ht1_hi_done, b, ht1_ready)
                norm1(2)
                transposed_lo(1, ht1_hi_done, b, ht1_ready)
                norm1(3)
                for g in range(NG):
                    if 1 <= g < NG - 1:
                        transposed_lo(g + 1, ht1_hi_done, b, ht1_ready)
                    l1_low(2 * g)
                    l1_low(2 * g + 1)
                for i in range(NT):
                    s = i % 2
                    if i + 2 < NT:
                        diag(i + 2)
                    if not last and i < EARLY:
                        t_unit(b + 1, i)
                    dve.wait_ge(acc_full, b * PHASES + 2 * NT + i + 1)
                    nc.vector.scalar_tensor_tensor(out=z_tmp[:, s, :], in0=acc[:, s, 0:D], scalar=dh[:, i:i + 1],
                                                   in1=bias1[:, :], op0=ALU.mult, op1=ALU.add).then_inc(z_tmp_done, 1)
                    dve.wait_ge(z_tmp_done, b * NT + i + 3)
                    dve.wait_ge(stored[s], 16 * (b * (NT // 2) + i // 2 + 1))
                    nc.vector.scalar_tensor_tensor(out=o_tile[:, s, :], in0=z_tmp[:, s, :], scalar=0.0,
                                                   in1=x1[:, i, :], op0=ALU.max, op1=ALU.add).then_inc(o_ready, 1)

            dve.wait_ge(h0_loaded, 16)
            for t in range(NT):
                stats_of(t, h0, stats0)
            moments(0, mv0, ve0, stats0, mean0, ve0_ready)
            dve.wait_ge(rstd0_ready, 1)
            for t in range(NT):
                norm(t, h0[:, t, :], h0, mv0, rstd0, h0_ready)
            layer0_dense(0)
            for u in range(EARLY):
                t_unit(0, u)
            with nc.vector.Fori(0, B - 1) as b:
                batch(b, False)
            batch(B - 1, True)

        @block.tensor
        def _(pe):
            pe.wait_ge(loaded_c, 16 * 8)
            pe.wait_ge(setup, 1)
            aw_v = aw_s[:, :].rearrange("p (c k) -> p k c", k=KD)
            for m in range(KD + 1):
                for k in range(KD):
                    w = wvt_raw[:, k, m * P:(m + 1) * P] if m < KD else bv_r[:, k, :]
                    ins = nc.tensor.matmul(db[:, 2 * m:2 * m + 2], w, aw_v[:, k, :], start=(k == 0), stop=(k == KD - 1))
            ins.then_inc(v_ready, 1)
            pe.wait_ge(ident_ready, 1)
            pe.wait_ge(weights_ready, 2)

            def transposes(g, tile, full):
                for s in range(2):
                    for k in range(KD):
                        ins = nc.tensor.transpose(tp[:, g % 2, k, s * P:(s + 1) * P],
                                                  tile(g, s)[:, k * P:(k + 1) * P], ident[:, :])
                ins.then_inc(full, 1)

            def split_product(dst, n, pairs):
                for c, (l_hi, l_lo, r_hi, r_lo) in enumerate(pairs):
                    for a, (l, r) in enumerate(((l_hi, r_hi), (l_hi, r_lo), (l_lo, r_hi))):
                        ins = nc.tensor.matmul(dst[:, 0:n], l, r, start=(c == 0 and a == 0),
                                               stop=(c == len(pairs) - 1 and a == 2))
                return ins

            def ht(part, g, k, s):
                return part[:, g % 2, k, s * P:(s + 1) * P]

            def layer0_dense(b):
                def tile(g, s):
                    return h0[:, 2 * g + s, :]

                def group(g):
                    pe.wait_ge(h0_ready, b * NT + 2 * g + 2)
                    transposes(g, tile, tp0_full)

                group(0)
                for g in range(NG):
                    if g + 1 < NG:
                        group(g + 1)
                    pe.wait_ge(ht0_ready, b * NG + g + 1)
                    pe.wait_ge(si_ready, b * NG + g)
                    split_product(ps, 2 * P, [(vi_hi[:, k, :], vi_lo[:, k, :], ht_hi[:, g % 2, k, :],
                                               ht_lo[:, g % 2, k, :]) for k in range(KD)]).then_inc(si_full, 1)
                    for s in range(2):
                        t = 2 * g + s
                        if t >= 2:
                            pe.wait_ge(g2_ready, b * NT + t - 1)
                        split_product(da[:, t % 2], 2 * D, [(ht(ht_hi, g, k, s), ht(ht_lo, g, k, s), wa_hi[:, k, :],
                                                             wa_lo[:, k, :]) for k in range(KD)]).then_inc(da_full, 1)
                        pe.wait_ge(p0_ready, b * NT + t)
                        split_product(db, D + 2, [(ht(ht_hi, g, k, s), ht(ht_lo, g, k, s), wb_hi[:, k, :],
                                                   wb_lo[:, k, :]) for k in range(KD)]).then_inc(db_full, 1)

            def layer1_dense(b, last):
                def tile(g, s):
                    return h1[:, g % 2, s, :]

                def group(g):
                    pe.wait_ge(h1_ready, b * NT + 2 * g + 2)
                    transposes(g, tile, tp1_full)

                group(0)
                for g in range(NG):
                    if g + 1 < NG:
                        group(g + 1)
                    pe.wait_ge(ht1_ready, b * NG + g + 1)
                    for s in range(2):
                        t = 2 * g + s
                        if t >= 2:
                            pe.wait_ge(y_ready, b * NT + t - 1)
                        elif not last:
                            pe.wait_ge(g2_ready, b * NT + 2 * NT + t - 1)
                        split_product(da[:, t % 2], D, [(ht(ht_hi, g, k, s), ht(ht_lo, g, k, s), wl_hi[:, k, :],
                                                         wl_lo[:, k, :]) for k in range(KD)]).then_inc(l1_full, 1)

            def accumulate(b, i, read, before, ready, n, lhs, rhs):
                s = i % 2
                if i >= 2:
                    pe.wait_ge(read, b * NT + i - 1 + 2 * (read is z_tmp_done))
                elif before is z_tmp_done:
                    pe.wait_ge(before, b * NT + i + 1)
                else:
                    pe.wait_ge(before, b * NT + NT + i - 1)
                for jt in range(NT):
                    if ready is not None and i == 0:
                        pe.wait_ge(ready, b * NT + jt + 1)
                    l_hi, l_lo = lhs(i, jt)
                    r_hi, r_lo = rhs(jt)
                    nc.tensor.matmul(acc[:, s, 0:n], l_hi, r_hi, start=(jt == 0), stop=False)
                    nc.tensor.matmul(acc[:, s, 0:D], l_hi, r_lo, start=False, stop=False)
                    ins = nc.tensor.matmul(acc[:, s, 0:n], l_lo, r_hi, start=False, stop=(jt == NT - 1))
                ins.then_inc(acc_full, 1)

            def of_t(i, jt):
                return t_hi[:, i, jt, :], t_lo[:, i, jt, :]

            def of_a(i, jt):
                return a_hi[:, i % 2, jt, :], a_lo[:, i % 2, jt, :]

            def batch(b, last):
                pe.wait_ge(g2_ready, b * NT + NT)
                for i in range(NT):
                    if i % 2 == 0:
                        pe.wait_ge(t_ready, b * NU + i + 2)
                    accumulate(b, i, g1_tmp_ready, z_tmp_done, None, D + 2, of_t, lambda jt: (g2_hi[:, jt, :], g2_lo[:, jt, :]))
                for i in range(NT):
                    accumulate(b, i, v_tmp_done, g1_tmp_ready, g1_ready, D, of_t, lambda jt: (g1_hi[:, jt, :], g1_lo[:, jt, :]))
                if not last:
                    layer0_dense(b + 1)
                layer1_dense(b, last)
                for i in range(NT):
                    pe.wait_ge(a_ready, b * NT + NT + i + 1)
                    accumulate(b, i, z_tmp_done, v_tmp_done, y_ready, D, of_a, lambda jt: (g1_hi[:, jt, :], g1_lo[:, jt, :]))

            layer0_dense(0)
            with nc.tensor.Fori(0, B - 1) as b:
                batch(b, False)
            batch(B - 1, True)


def kernel(x, adj, L0_gnn_Wv, L0_gnn_bv, L0_gnn_aw, L0_gnn_ab, L0_gnn_Wk, L0_gnn_bk, L1_gnn_kernel, L1_gnn_bias):
    import concourse.bacc as bacc
    from concourse.bass_utils import run_bass_kernel_spmd

    x, adj = np.asarray(x), np.asarray(adj)
    B, N, D = x.shape
    P = 128
    nt = N // P
    adj_t = adj.reshape(B, nt // 2, 2, P, 2, nt // 2, P).transpose(0, 1, 4, 6, 2, 5, 3)
    adj_t = np.ascontiguousarray(adj_t).reshape(B, nt // 2, 2, P, 2, nt // 2 * P)
    arrays = {
        "x": x,
        "adj": adj,
        "adj_t": adj_t,
        "wv_t": np.ascontiguousarray(np.asarray(L0_gnn_Wv).T),
        "bv": np.asarray(L0_gnn_bv),
        "aw": np.asarray(L0_gnn_aw),
        "ab": np.asarray(L0_gnn_ab),
        "wk": np.asarray(L0_gnn_Wk),
        "bk": np.asarray(L0_gnn_bk),
        "w_l1": np.asarray(L1_gnn_kernel),
        "bias_l1": np.asarray(L1_gnn_bias),
    }
    arrays = {f"{k}_dram": np.ascontiguousarray(a) for k, a in arrays.items()}
    nc = bacc.Bacc("TRN2", target_bir_lowering=False, num_devices=1, dynamic_dma_scratch_size=1024)
    args = [nc.dram_tensor(k, a.shape, mybir.dt.from_np(a.dtype), kind="ExternalInput").ap()
            for k, a in arrays.items()]
    out = nc.dram_tensor("out_dram", (B, N, D), F32, kind="ExternalOutput").ap()
    gnn_two_layers(nc, *args, out)
    r = run_bass_kernel_spmd(nc, [arrays], core_ids=[0])
    return r.results[0]["out_dram"]
```

```python
import numpy as np
import concourse.bass as bass
from concourse import mybir
from contextlib import ExitStack

F32 = mybir.dt.float32
F32R = mybir.dt.float32r
ALU = mybir.AluOpType
ACT = mybir.ActivationFunctionType



def gnn_two_layers(nc, x, adj, adj_t, wv_t, bv, aw, ab, wk, bk, w_l1, bias_l1, out):
    B, N, D = x.shape
    P = 128
    NT = N // P
    KD = D // P
    NG = NT // 2
    NU = NT
    HJ = NT // 2
    HALVES = [(k, h) for k in range(NU + 1) for h in range(2)]
    T_V = {i: [HALVES[i]] for i in range(6)}
    T_Z = {i: [HALVES[i + 6]] for i in range(8)}
    T_U = {i: [HALVES[i + 14]] for i in range(4)}
    TS, RS = 2, 4
    PHASES = 3 * NT
    EPS_LN, EPS_ROW, SLOPE = 1e-5, 1e-12, 0.2

    ctx = ExitStack()
    with ctx:
        def sb(name, shape, dt=F32):
            return ctx.enter_context(nc.sbuf_tensor(name, shape, dt))

        def pb(name, shape):
            return ctx.enter_context(nc.psum_tensor(name, shape, F32))

        def sem(name):
            return ctx.enter_context(nc.semaphore(name))

        t_hi = sb("t_hi", [P, NT, NT, P], F32R)
        t_lo = sb("t_lo", [P, NT, NT, P], F32R)
        tg_a = sb("tg_a", [P, TS, 2, HJ, P])
        tg_e = sb("tg_e", [P, TS, 2, HJ, P])
        a_raw = sb("a_raw", [P, RS, N])
        a_hi = sb("a_hi", [P, 2, NT, P], F32R)
        a_lo = sb("a_lo", [P, 2, NT, P], F32R)
        wa_hi = sb("wa_hi", [P, KD, 2 * D], F32R)
        wa_lo = sb("wa_lo", [P, KD, 2 * D], F32R)
        wb_hi = sb("wb_hi", [P, KD, D + 2], F32R)
        wb_lo = sb("wb_lo", [P, KD, D + 2], F32R)
        wl_hi = sb("wl_hi", [P, KD, D], F32R)
        wl_lo = sb("wl_lo", [P, KD, D], F32R)
        vi_hi = sb("vi_hi", [P, KD, P], F32R)
        vi_lo = sb("vi_lo", [P, KD, P], F32R)
        h0 = sb("h0", [P, NT, D])
        h1 = sb("h1", [P, 2, 2, D])
        x_res = sb("x_res", [P, 2, D])
        ht_hi = sb("ht_hi", [P, 2, KD, 2 * P], F32R)
        ht_lo = sb("ht_lo", [P, 2, KD, 2 * P], F32R)
        p0 = sb("p0", [P, 2, NT, D])
        p1 = sb("p1", [P, NT, D])
        g2_hi = sb("g2_hi", [P, NT, D + 2], F32R)
        g2_lo = sb("g2_lo", [P, NT, D], F32R)
        g1_hi = sb("g1_hi", [P, NT, D], F32R)
        g1_lo = sb("g1_lo", [P, NT, D], F32R)
        g1_tmp = sb("g1_tmp", [P, 2, D])
        si = sb("si", [P, N])
        sj = sb("sj", [P, NT])
        z_tmp = sb("z_tmp", [P, 2, D])
        o_tile = sb("o_tile", [P, 2, D])
        bk_sum = sb("bk_sum", [P, D])
        bias1 = sb("bias1", [P, D])
        ident = sb("ident", [P, P])
        st = sb("st", [P, NT, 6])
        mv0 = sb("mv0", [P, NT, 2])
        mv1 = sb("mv1", [P, NT, 2])
        ve0 = sb("ve0", [P, NT])
        ve1 = sb("ve1", [P, NT])
        rstd0 = sb("rstd0", [P, NT])
        rstd1 = sb("rstd1", [P, NT])
        row_a = sb("row_a", [P, NT])
        row_a1 = sb("row_a1", [P, NT])
        dh = sb("dh", [P, NT])
        mhalf = sb("mhalf", [P, NT])
        row_t = sb("row_t", [P, NT])
        rinv = sb("rinv", [P, NT])
        aw_s = sb("aw_s", [P, 2 * KD])
        bv_s = sb("bv_s", [P, KD])
        ab_s = sb("ab_s", [P, 1])
        bv_r = sb("bv_r", [P, KD, P])
        v_s = sb("v_s", [P, KD + 1, 2])
        cst = sb("cst", [P, 2])

        wk_raw = p0[:, 1].rearrange("p (a k) n -> p a k n", k=KD)
        wvt_raw = p1[:, 0:KD, :]
        bk_raw = p0[:, 0, 0:3, :]

        tp = pb("tp", [P, 2, KD, 2 * P])
        da = pb("da", [P, 2, 2 * D])
        db = pb("db", [P, 512])
        ps = pb("ps", [P, 512])
        acc = pb("acc", [P, 2, 512])

        l1_bank = [da[:, 0, :], da[:, 1, :], db[:, :], ps[:, :]]

        loaded_c = sem("loaded_c")
        setup = sem("setup")
        ident_zero = sem("ident_zero")
        ident_ready = sem("ident_ready")
        v_ready = sem("v_ready")
        weights_ready = sem("weights_ready")
        h0_loaded = sem("h0_loaded")
        x_res_loaded = [sem(f"x_res_loaded{s}") for s in range(2)]
        tg_loaded = [sem(f"tg_loaded{s}") for s in range(TS)]
        raw_loaded = [sem(f"raw_loaded{s}") for s in range(RS)]
        stored = [sem(f"stored{s}") for s in range(2)]
        tp0_full, tp1_full = sem("tp0_full"), sem("tp1_full")
        si_full = sem("si_full")
        da_full, db_full, l1_full = sem("da_full"), sem("db_full"), sem("l1_full")
        acc_full = sem("acc_full")
        ht0_hi_done, ht1_hi_done = sem("ht0_hi_done"), sem("ht1_hi_done")
        ht0_ready, ht1_ready = sem("ht0_ready"), sem("ht1_ready")
        si_ready = sem("si_ready")
        g2_hi_done, g2_ready = sem("g2_hi_done"), sem("g2_ready")
        p0_ready = sem("p0_ready")
        score_done, leaky_done, e_ready = sem("score_done"), sem("leaky_done"), sem("e_ready")
        prod_ready = sem("prod_ready")
        t_hi_done, t_ready = sem("t_hi_done"), sem("t_ready")
        row_t_done, rinv_done = sem("row_t_done"), sem("rinv_done")
        g1_tmp_ready, g1_hi_done, g1_ready = sem("g1_tmp_ready"), sem("g1_hi_done"), sem("g1_ready")
        rows_done, rows1_done, dh_ready = sem("rows_done"), sem("rows1_done"), sem("dh_ready")
        stats0, mean0, ve0_ready, rstd0_ready = (sem(n) for n in ("stats0", "mean0", "ve0_ready", "rstd0_ready"))
        stats1, mean1, ve1_ready, rstd1_ready = (sem(n) for n in ("stats1", "mean1", "ve1_ready", "rstd1_ready"))
        stats_seen = sem("stats_seen")
        h0_ready, h1_ready = sem("h0_ready"), sem("h1_ready")
        v_tmp_done, x1_ready = sem("v_tmp_done"), sem("x1_ready")
        y_hi_done, y_ready = sem("y_hi_done"), sem("y_ready")
        diag_done, a_hi_done, a_ready = sem("diag_done"), sem("a_hi_done"), sem("a_ready")
        z_tmp_done, o_ready = sem("z_tmp_done"), sem("o_ready")

        x_v = x.rearrange("b (t p) d -> b p t d", p=P)
        out_v = out.rearrange("b (t p) d -> b p t d", p=P)
        adj_v = adj.rearrange("b (t p) j -> b p t j", p=P)

        def chunk(src, b, i):
            return src[b, i // 2, :, :, i % 2].rearrange("h p c -> p h c")

        def t_view(t, u):
            cp, jh = u // 2, u % 2
            return t[:, 2 * cp:2 * cp + 2, jh * HJ:(jh + 1) * HJ, :]

        def a_half(part, i, h):
            return part[:, i % 2, h * HJ:(h + 1) * HJ].rearrange("p q i -> p (q i)")

        def load_t_unit(eng, b, u):
            eng.dma_start(tg_a[:, u % TS].rearrange("p s q i -> p (s q i)"),
                          adj_t[b, u // 2, u % 2].rearrange("p s c -> p (s c)")).then_inc(tg_loaded[u % TS], 16)

        def next_unit(b, u, last):
            if u + TS < NU:
                return b, u + TS
            return None if last else (b + 1, u + TS - NU)

        block = ctx.enter_context(nc.Block())

        @block.sync
        def _(sp):
            sp.dma_start(h0[:, :, :], x_v[0]).then_inc(h0_loaded, 16)
            sp.dma_start(wk_raw[:, 0:3], wk.rearrange("a (k p) n -> p a k n", p=P)).then_inc(loaded_c, 16)
            sp.dma_start(wk_raw[:, 3], w_l1.rearrange("(k p) n -> p k n", p=P)).then_inc(loaded_c, 16)
            sp.dma_start(wvt_raw, wv_t.rearrange("(k p) n -> p k n", p=P)).then_inc(loaded_c, 16)
            sp.dma_start(bk_raw, bk.rearrange("(o a) n -> o a n", o=1).to_broadcast([P, 3, D])).then_inc(loaded_c, 16)
            sp.dma_start(bias1[:, :], bias_l1.rearrange("(o n) -> o n", o=1).to_broadcast([P, D])).then_inc(loaded_c, 16)
            with nc.allow_non_contiguous_dma(reason="three short vectors"):
                sp.dma_start(aw_s[:, :], aw.rearrange("(c p) o -> p (c o)", p=P)).then_inc(loaded_c, 16)
                sp.dma_start(bv_s[:, :], bv.rearrange("(c p) -> p c", p=P)).then_inc(loaded_c, 16)
                sp.dma_start(ab_s[:, :], ab.rearrange("(o n) -> o n", o=1).to_broadcast([P, 1])).then_inc(loaded_c, 16)
            def rows(b):
                for t in range(NT):
                    if t < RS:
                        sp.wait_ge(a_ready, 2 * (b * NT + NT - RS + t + 1))
                    else:
                        sp.wait_ge(rows_done, b * NT + t - RS + 1)
                    sp.dma_start(a_raw[:, t % RS, :], adj_v[b, :, t]).then_inc(raw_loaded[t % RS], 16)

            def stores(b, i):
                sp.wait_ge(o_ready, b * NT + i + 1)
                sp.dma_start(out_v[b, :, i], o_tile[:, i % 2, :]).then_inc(stored[i % 2], 16)

            def load_chunk(b, i):
                if i < RS:
                    sp.wait_ge(rows_done, b * NT + NT - RS + i + 1)
                else:
                    sp.wait_ge(a_ready, 2 * (b * NT + i - RS + 1 + NT))
                sp.dma_start(a_raw[:, i % RS, :].rearrange("p (h c) -> p h c", h=2),
                             chunk(adj_t, b, i)).then_inc(raw_loaded[i % RS], 16)

            def batch(b, last):
                if not last:
                    sp.wait_ge(tp0_full, b * NG + NG)
                    sp.dma_start(h0[:, :, :], x_v[b + 1]).then_inc(h0_loaded, 16)
                rows(b)
                for i in range(RS):
                    load_chunk(b, i)
                for i in range(NT):
                    sp.wait_ge(x1_ready, b * NT + i + 1)
                    sp.dma_start(x_res[:, i % 2, :], x_v[b, :, i]).then_inc(x_res_loaded[i % 2], 16)
                for i in range(RS, NT):
                    load_chunk(b, i)
                    stores(b, i - RS)
                for i in range(NT - RS, NT):
                    stores(b, i)

            with nc.sync.Fori(0, B - 2, 2) as b:
                batch(b, False)
                batch(b + 1, False)
            batch(B - 2, False)
            batch(B - 1, True)
            for s in range(2):
                sp.wait_ge(stored[s], 16 * (B * NT // 2 + 1))

        @block.gpsimd
        def _(pool):
            pool.sem_inc(a_ready, 2 * NT)
            nc.gpsimd.memset(mhalf[:, :], -0.5)
            nc.gpsimd.memset(ident[:, :], 0.0).then_inc(ident_zero, 1)
            pool.wait_ge(ident_zero, 1)
            nc.gpsimd.affine_select(out=ident[:, :], in_=ident[:, :], compare_op=ALU.not_equal, fill=1.0,
                                    base=0, pattern=[[-1, P]], channel_multiplier=1).then_inc(ident_ready, 1)

            def power(dst, src, ready, count, done, c=slice(0, NT)):
                pool.wait_ge(ready, count)
                nc.gpsimd.tensor_tensor(dst[:, c], src[:, c], mhalf[:, c], ALU.pow).then_inc(done, 1)

            def g1_split(b, i):
                pool.wait_ge(g1_hi_done, b * NT + i + 1)
                nc.gpsimd.tensor_tensor(g1_lo[:, i, :], g1_tmp[:, i % 2, :], g1_hi[:, i, :].bitcast(F32),
                                        ALU.subtract).then_inc(g1_ready, 1)

            def a_split(b, i):
                for h in range(2):
                    pool.wait_ge(a_hi_done, 2 * (b * NT + i) + h + 1)
                    nc.gpsimd.tensor_tensor(a_half(a_lo, i, h), a_raw[:, i % RS, h * N // 2:(h + 1) * N // 2],
                                            a_half(a_hi, i, h).bitcast(F32), ALU.subtract).then_inc(a_ready, 1)

            def batch(b, last):
                for i in range(NT):
                    g1_split(b, i)
                    if i == 3 and not last:
                        power(rstd0, ve0, ve0_ready, b + 2, rstd0_ready)
                power(dh, row_a1, rows1_done, b + 1, dh_ready)
                for g in range(NG):
                    power(rstd1, ve1, ve1_ready, b * NG + g + 1, rstd1_ready, slice(2 * g, 2 * g + 2))
                    if g < 2:
                        a_split(b, g)
                for i in range(2, NT):
                    a_split(b, i)

            power(rstd0, ve0, ve0_ready, 1, rstd0_ready)
            with nc.gpsimd.Fori(0, B - 2, 2) as b:
                batch(b, False)
                batch(b + 1, False)
            batch(B - 2, False)
            batch(B - 1, True)

        @block.scalar
        def _(act):
            load_t_unit(act, 0, 0)
            load_t_unit(act, 0, 1)

            def transposed_hi(g, full, b, done):
                act.wait_ge(full, b * NG + g + 1)
                nc.scalar.activation(ht_hi[:, g % 2], tp[:, g % 2], ACT.Relu).then_inc(done, 1)

            def dense0(b, t):
                act.wait_ge(da_full, b * NT + t + 1)
                nc.scalar.copy(p1[:, t, :], da[:, t % 2, 0:D])
                nc.scalar.copy(g2_hi[:, t, 0:D], da[:, t % 2, D:2 * D]).then_inc(g2_hi_done, 1)

            def si_copy(b, g):
                act.wait_ge(si_full, b * NG + g + 1)
                nc.scalar.copy(si[:, g * 2 * P:(g + 1) * 2 * P], ps[:, 0:2 * P]).then_inc(si_ready, 1)

            def t_step(b, k, half, last, first=False):
                s = k % TS
                if half == 0 and k < NU:
                    if not (first and k < TS):
                        act.wait_ge(t_ready, b * NU + k - TS + 1)
                    c = slice(k // 2 * 2 * P, (k // 2 + 1) * 2 * P)
                    for q in range(HJ):
                        jt = k % 2 * HJ + q
                        ins = nc.scalar.activation(tg_e[:, s, :, q, :], si[:, c].rearrange("p (s i) -> p s i", s=2),
                                                   ACT.Identity, bias=sj[:, jt:jt + 1])
                    ins.then_inc(score_done, 1)
                if half == 1 and k > 0:
                    u = k - 1
                    if not first:
                        act.wait_ge(acc_full, (b - 1) * PHASES + NT + 2 * (u // 2) + 2)
                    act.wait_ge(prod_ready, b * NU + u + 1)
                    nc.scalar.copy(t_view(t_hi, u), tg_e[:, u % TS]).then_inc(t_hi_done, 1)
                    nxt = next_unit(b, u, last)
                    if nxt is not None:
                        load_t_unit(act, *nxt)
                if half == 1 and k < NU:
                    act.wait_ge(leaky_done, b * NU + k + 1)
                    nc.scalar.activation(tg_e[:, s], tg_e[:, s], ACT.Exp).then_inc(e_ready, 1)

            def layer0_dense(b):
                for g in range(NG):
                    if g + 1 < NG:
                        transposed_hi(g + 1, tp0_full, b, ht0_hi_done)
                    si_copy(b, g)
                    dense0(b, 2 * g)
                    dense0(b, 2 * g + 1)

            def rows(b, t):
                act.wait_ge(raw_loaded[t % RS], 16 * (b * (2 * NT // RS) + t // RS + 1))
                nc.scalar.activation(a_raw[:, t % RS, :], a_raw[:, t % RS, :], ACT.Copy,
                                     accum_out=row_a[:, t:t + 1]).then_inc(rows_done, 1)

            def l1_scaled(b, t):
                act.wait_ge(l1_full, b * NT + t + 1)
                nc.scalar.activation(g1_hi[:, t, :], l1_bank[t % 4][:, 0:D], ACT.Copy,
                                     scale=dh[:, t:t + 1]).then_inc(y_hi_done, 1)

            def a_round(b, i):
                act.wait_ge(diag_done, b * NT + i + 1)
                if i >= 2:
                    act.wait_ge(acc_full, b * PHASES + 2 * NT + i - 1)
                for h in range(2):
                    nc.scalar.copy(a_half(a_hi, i, h), a_raw[:, i % RS, h * N // 2:(h + 1) * N // 2]).then_inc(a_hi_done, 1)

            def batch(b, last):
                for i in range(NT):
                    if i == NT - 1 and not last:
                        transposed_hi(0, tp0_full, b + 1, ht0_hi_done)
                    act.wait_ge(g1_tmp_ready, b * NT + i + 1)
                    nc.scalar.copy(g1_hi[:, i, :], g1_tmp[:, i % 2, :]).then_inc(g1_hi_done, 1)
                    for step in T_U.get(i, ()):
                        t_step(b, *step, last, first=True)
                    if i >= 1:
                        rows(b, i - 1)
                rows(b, NT - 1)
                if not last:
                    layer0_dense(b + 1)
                for i in range(NT):
                    if i in (1, 3):
                        a_round(b, i // 2)
                    if not last:
                        for step in T_V.get(i, ()):
                            t_step(b + 1, *step, False)
                    if i == 6:
                        transposed_hi(0, tp1_full, b, ht1_hi_done)
                    if i == 7:
                        transposed_hi(1, tp1_full, b, ht1_hi_done)
                act.wait_ge(dh_ready, b + 1)
                for g in range(NG):
                    if g in (1, 2):
                        transposed_hi(g + 1, tp1_full, b, ht1_hi_done)
                    l1_scaled(b, 2 * g)
                    l1_scaled(b, 2 * g + 1)
                for i in range(NT):
                    if i + 2 < NT:
                        a_round(b, i + 2)
                    if not last:
                        for step in T_Z.get(i, ()):
                            t_step(b + 1, *step, False)

            transposed_hi(0, tp0_full, 0, ht0_hi_done)
            layer0_dense(0)
            for step in HALVES[:14]:
                t_step(0, *step, False, first=True)
            with nc.scalar.Fori(0, B - 2, 2) as b:
                batch(b, False)
                batch(b + 1, False)
            batch(B - 2, False)
            batch(B - 1, True)

        @block.vector
        def _(dve):
            dve.sem_inc(z_tmp_done, 2)
            for s in range(2):
                dve.sem_inc(stored[s], 16)
            dve.sem_inc(x1_ready, 2)
            steps = [0]

            def then(ins):
                steps[0] += 1
                ins.then_inc(setup, 1)
                dve.wait_ge(setup, steps[0])

            dve.wait_ge(loaded_c, 16 * 8)
            nc.vector.memset(g2_hi[:, :, D:D + 2].bitcast(F32), 1.0)
            nc.vector.memset(wb_hi[:, :, D + 1:D + 2].bitcast(F32), 0.0)
            nc.vector.memset(wb_lo[:, :, D + 1:D + 2].bitcast(F32), 0.0)
            nc.vector.tensor_tensor(bk_sum[:, :], bk_raw[:, 0, :], bk_raw[:, 1, :], ALU.add)
            for k in range(KD):
                nc.vector.tensor_copy(bv_r[:, k, :], bv_s[:, k:k + 1].to_broadcast([P, P]))
            for a in range(2):
                nc.vector.tensor_copy(wa_hi[:, :, a * D:(a + 1) * D], wk_raw[:, a + 1])
            nc.vector.tensor_copy(wb_hi[:, :, 0:D], wk_raw[:, 0])
            then(nc.vector.tensor_copy(wl_hi[:, :, :], wk_raw[:, 3]))
            nc.vector.tensor_tensor(bk_sum[:, :], bk_sum[:, :], bk_raw[:, 2, :], ALU.add)
            for a in range(2):
                nc.vector.tensor_tensor(wa_lo[:, :, a * D:(a + 1) * D], wk_raw[:, a + 1],
                                        wa_hi[:, :, a * D:(a + 1) * D].bitcast(F32), ALU.subtract)
            nc.vector.tensor_tensor(wb_lo[:, :, 0:D], wk_raw[:, 0], wb_hi[:, :, 0:D].bitcast(F32), ALU.subtract)
            nc.vector.tensor_tensor(wl_lo[:, :, :], wk_raw[:, 3], wl_hi[:, :, :].bitcast(F32),
                                    ALU.subtract).then_inc(weights_ready, 1)
            dve.wait_ge(v_ready, 1)
            then(nc.vector.tensor_copy(v_s[:, :, :], db[:, 0:2 * (KD + 1)].rearrange("p (k c) -> p k c", c=2)))
            nc.vector.tensor_tensor(cst[:, 0:1], v_s[:, KD, 0:1], v_s[:, KD, 1:2], ALU.add)
            nc.vector.tensor_copy(wb_hi[:, :, D:D + 1], v_s[:, 0:KD, 0:1])
            for k in range(KD):
                ins = nc.vector.tensor_copy(vi_hi[:, k, :], v_s[:, k, 1:2].to_broadcast([P, P]))
            then(ins)
            nc.vector.tensor_tensor(cst[:, 1:2], cst[:, 0:1], ab_s[:, :], ALU.add)
            nc.vector.tensor_tensor(wb_lo[:, :, D:D + 1], v_s[:, 0:KD, 0:1], wb_hi[:, :, D:D + 1].bitcast(F32),
                                    ALU.subtract)
            for k in range(KD):
                ins = nc.vector.tensor_tensor(vi_lo[:, k, :], v_s[:, k, 1:2].to_broadcast([P, P]),
                                              vi_hi[:, k, :].bitcast(F32), ALU.subtract)
            ins.then_inc(weights_ready, 1)

            def moments(count, mv, ve, stats, mean, ve_ready, tiles):
                dve.wait_ge(stats, count)
                dve.sem_inc(stats_seen, 1)
                for t in tiles:
                    ins = nc.vector.bn_aggr(mv[:, t, :], st[:, t, :])
                ins.then_inc(mean, 1)
                dve.wait_ge(mean, count)
                c = slice(tiles[0], tiles[-1] + 1)
                nc.vector.tensor_scalar_add(ve[:, c], mv[:, c, 1], EPS_LN).then_inc(ve_ready, 1)

            def stats0_of(t):
                ins = nc.vector.bn_stats(st[:, t, :], h0[:, t, :])
                if t == NT - 1:
                    ins.then_inc(stats0, 1)

            def moments0(count):
                moments(count, mv0, ve0, stats0, mean0, ve0_ready, range(NT))

            def norm(dst, src, t, mv, rstd, ready):
                nc.vector.tensor_scalar(dst, src, mv[:, t, 0:1], rstd[:, t:t + 1],
                                        ALU.subtract, ALU.mult).then_inc(ready, 1)

            def norm0(g):
                for t in (2 * g, 2 * g + 1):
                    norm(h0[:, t, :], h0[:, t, :], t, mv0, rstd0, h0_ready)

            def norm1(b, par, g):
                dve.wait_ge(rstd1_ready, b * NG + g + 1)
                if g >= 2:
                    dve.wait_ge(tp1_full, b * NG + g - 1)
                for s in range(2):
                    norm(h1[:, g % 2, s, :], p0[:, par, 2 * g + s, :], 2 * g + s, mv1, rstd1, h1_ready)

            def transposed_lo(g, hi_done, b, ready):
                dve.wait_ge(hi_done, b * NG + g + 1)
                nc.vector.scalar_tensor_tensor(out=ht_lo[:, g % 2], in0=tp[:, g % 2], scalar=0.0,
                                               in1=ht_hi[:, g % 2].bitcast(F32),
                                               op0=ALU.max, op1=ALU.subtract).then_inc(ready, 1)

            def dense0(b, par, t):
                dve.wait_ge(g2_hi_done, b * NT + t + 1)
                nc.vector.tensor_tensor(g2_lo[:, t, :], da[:, t % 2, D:2 * D], g2_hi[:, t, 0:D].bitcast(F32),
                                        ALU.subtract).then_inc(g2_ready, 1)
                dve.wait_ge(db_full, b * NT + t + 1)
                nc.vector.tensor_tensor(p0[:, par, t, :], db[:, 0:D], bk_sum[:, :], ALU.add)
                nc.vector.tensor_tensor(sj[:, t:t + 1], db[:, D:D + 1], cst[:, 1:2], ALU.add).then_inc(p0_ready, 1)

            def layer0_dense(b, par):
                for g in range(NG):
                    if g + 1 < NG:
                        transposed_lo(g + 1, ht0_hi_done, b, ht0_ready)
                    if g + 2 < NG:
                        norm0(g + 2)
                    dense0(b, par, 2 * g)
                    dense0(b, par, 2 * g + 1)

            def t_step(b, k, half):
                u, s = k - 1, (k - 1) % TS
                if half == 0 and k > 0:
                    dve.wait_ge(e_ready, b * NU + u + 1)
                    dve.wait_ge(tg_loaded[s], 16 * (b * (NU // TS) + u // TS + 1))
                    nc.vector.tensor_tensor(tg_e[:, s], tg_a[:, s], tg_e[:, s], ALU.mult).then_inc(prod_ready, 1)
                if half == 1 and k < NU:
                    dve.wait_ge(score_done, b * NU + k + 1)
                    e = tg_e[:, k % TS]
                    nc.vector.scalar_tensor_tensor(out=e, in0=e, scalar=SLOPE, in1=e,
                                                   op0=ALU.mult, op1=ALU.max).then_inc(leaky_done, 1)
                if half == 1 and k > 0:
                    dve.wait_ge(t_hi_done, b * NU + u + 1)
                    nc.vector.tensor_tensor(t_view(t_lo, u), tg_e[:, s], t_view(t_hi, u).bitcast(F32),
                                            ALU.subtract).then_inc(t_ready, 1)

            def u_chunk(b, i):
                s = i % 2
                dve.wait_ge(acc_full, b * PHASES + i + 1)
                nc.vector.tensor_scalar_add(row_t[:, i:i + 1], acc[:, s, D:D + 1], EPS_ROW).then_inc(row_t_done, 1)
                dve.wait_ge(row_t_done, b * NT + i + 1)
                nc.vector.reciprocal(rinv[:, i:i + 1], row_t[:, i:i + 1]).then_inc(rinv_done, 1)
                dve.wait_ge(rinv_done, b * NT + i + 1)
                if i >= 2:
                    dve.wait_ge(g1_ready, b * NT + i - 1)
                nc.vector.scalar_tensor_tensor(out=g1_tmp[:, s, :], in0=acc[:, s, 0:D], scalar=rinv[:, i:i + 1],
                                               in1=p1[:, i, :], op0=ALU.mult, op1=ALU.add).then_inc(g1_tmp_ready, 1)

            def v_chunk(b, par, i):
                s, x1 = i % 2, p0[:, par, i, :]
                dve.wait_ge(acc_full, b * PHASES + NT + i + 1)
                nc.vector.scalar_tensor_tensor(out=x1, in0=acc[:, s, 0:D], scalar=rinv[:, i:i + 1],
                                               in1=x1, op0=ALU.mult, op1=ALU.add).then_inc(v_tmp_done, 1)
                dve.wait_ge(v_tmp_done, b * NT + i + 1)
                dve.wait_ge(x_res_loaded[s], 16 * (b * (NT // 2) + i // 2 + 1))
                nc.vector.scalar_tensor_tensor(out=x1, in0=x1, scalar=0.0, in1=x_res[:, s, :],
                                               op0=ALU.max, op1=ALU.add).then_inc(x1_ready, 1)
                dve.wait_ge(x1_ready, b * NT + i + 3)
                ins = nc.vector.bn_stats(st[:, i, :], x1)
                if i % 2:
                    ins.then_inc(stats1, 1)

            def diag(b, i):
                dve.wait_ge(raw_loaded[i % RS], 16 * (b * (2 * NT // RS) + NT // RS + i // RS + 1))
                blk = a_raw[:, i % RS, i * P:(i + 1) * P]
                nc.vector.tensor_tensor(blk, blk, ident[:, :], ALU.add).then_inc(diag_done, 1)

            def l1_low(b, t):
                dve.wait_ge(y_hi_done, b * NT + t + 1)
                nc.vector.scalar_tensor_tensor(out=g1_lo[:, t, :], in0=l1_bank[t % 4][:, 0:D], scalar=dh[:, t:t + 1],
                                               in1=g1_hi[:, t, :].bitcast(F32), op0=ALU.mult, op1=ALU.subtract)\
                    .then_inc(y_ready, 1)

            def z_chunk(b, par, i):
                s = i % 2
                dve.wait_ge(acc_full, b * PHASES + 2 * NT + i + 1)
                nc.vector.scalar_tensor_tensor(out=z_tmp[:, s, :], in0=acc[:, s, 0:D], scalar=dh[:, i:i + 1],
                                               in1=bias1[:, :], op0=ALU.mult, op1=ALU.add).then_inc(z_tmp_done, 1)
                dve.wait_ge(z_tmp_done, b * NT + i + 3)
                dve.wait_ge(stored[s], 16 * (b * (NT // 2) + i // 2 + 1))
                nc.vector.scalar_tensor_tensor(out=o_tile[:, s, :], in0=z_tmp[:, s, :], scalar=0.0,
                                               in1=p0[:, par, i, :], op0=ALU.max, op1=ALU.add).then_inc(o_ready, 1)

            def batch(b, par, last):
                for i in range(NT):
                    if i == NT - 1 and not last:
                        transposed_lo(0, ht0_hi_done, b + 1, ht0_ready)
                    u_chunk(b, i)
                    for step in T_U.get(i, ()):
                        t_step(b, *step)
                    if not last:
                        if i == 0:
                            dve.wait_ge(h0_loaded, 16 * (b + 2))
                        if i < NG:
                            stats0_of(2 * i)
                            stats0_of(2 * i + 1)
                        if i == NG - 1:
                            moments0(b + 2)
                        if i == NT - 3:
                            dve.wait_ge(rstd0_ready, b + 2)
                            norm0(0)
                            norm0(1)
                dve.wait_ge(rows_done, b * NT + NT)
                nc.vector.tensor_scalar_add(row_a1[:, :], row_a[:, :], 1.0).then_inc(rows1_done, 1)
                if not last:
                    layer0_dense(b + 1, 1 - par)
                for i in range(NT):
                    if i in (0, 1):
                        diag(b, i)
                    if i == 6:
                        transposed_lo(0, ht1_hi_done, b, ht1_ready)
                    v_chunk(b, par, i)
                    if i % 2:
                        moments(b * NG + i // 2 + 1, mv1, ve1, stats1, mean1, ve1_ready, (i - 1, i))
                    elif i > 0:
                        norm1(b, par, i // 2 - 1)
                    if i == 6:
                        transposed_lo(1, ht1_hi_done, b, ht1_ready)
                    if not last:
                        for step in T_V.get(i, ()):
                            t_step(b + 1, *step)
                for g in range(NG):
                    l1_low(b, 2 * g)
                    l1_low(b, 2 * g + 1)
                    if g in (0, 1):
                        transposed_lo(g + 2, ht1_hi_done, b, ht1_ready)
                    if g == 0:
                        norm1(b, par, NG - 1)
                for i in range(NT):
                    if i + 2 < NT:
                        diag(b, i + 2)
                    z_chunk(b, par, i)
                    if not last:
                        for step in T_Z.get(i, ()):
                            t_step(b + 1, *step)

            dve.wait_ge(h0_loaded, 16)
            for t in range(NT):
                stats0_of(t)
            moments0(1)
            dve.wait_ge(rstd0_ready, 1)
            norm0(0)
            norm0(1)
            transposed_lo(0, ht0_hi_done, 0, ht0_ready)
            layer0_dense(0, 0)
            for step in HALVES[:14]:
                t_step(0, *step)
            with nc.vector.Fori(0, B - 2, 2) as b:
                batch(b, 0, False)
                batch(b + 1, 1, False)
            batch(B - 2, 0, False)
            batch(B - 1, 1, True)

        @block.tensor
        def _(pe):
            pe.wait_ge(loaded_c, 16 * 8)
            pe.wait_ge(setup, 1)
            aw_v = aw_s[:, :].rearrange("p (c k) -> p k c", k=KD)
            for m in range(KD + 1):
                for k in range(KD):
                    w = wvt_raw[:, k, m * P:(m + 1) * P] if m < KD else bv_r[:, k, :]
                    ins = nc.tensor.matmul(db[:, 2 * m:2 * m + 2], w, aw_v[:, k, :], start=(k == 0), stop=(k == KD - 1))
            ins.then_inc(v_ready, 1)
            pe.wait_ge(ident_ready, 1)
            pe.wait_ge(weights_ready, 2)

            def transposes(g, tile, full):
                for s in range(2):
                    for k in range(KD):
                        ins = nc.tensor.transpose(tp[:, g % 2, k, s * P:(s + 1) * P],
                                                  tile(g, s)[:, k * P:(k + 1) * P], ident[:, :])
                ins.then_inc(full, 1)

            def split_product(dst, n, pairs):
                for c, (l_hi, l_lo, r_hi, r_lo) in enumerate(pairs):
                    for a, (l, r) in enumerate(((l_hi, r_hi), (l_hi, r_lo), (l_lo, r_hi))):
                        ins = nc.tensor.matmul(dst[:, 0:n], l, r, start=(c == 0 and a == 0),
                                               stop=(c == len(pairs) - 1 and a == 2))
                return ins

            def ht(part, g, k, s):
                return part[:, g % 2, k, s * P:(s + 1) * P]

            def layer0_transposes(b, g):
                pe.wait_ge(h0_ready, b * NT + 2 * g + 2)
                transposes(g, lambda g, s: h0[:, 2 * g + s, :], tp0_full)

            def layer0_dense(b):
                for g in range(NG):
                    if g + 1 < NG:
                        layer0_transposes(b, g + 1)
                    pe.wait_ge(ht0_ready, b * NG + g + 1)
                    pe.wait_ge(si_ready, b * NG + g)
                    split_product(ps, 2 * P, [(vi_hi[:, k, :], vi_lo[:, k, :], ht_hi[:, g % 2, k, :],
                                               ht_lo[:, g % 2, k, :]) for k in range(KD)]).then_inc(si_full, 1)
                    for s in range(2):
                        t = 2 * g + s
                        if t >= 2:
                            pe.wait_ge(g2_ready, b * NT + t - 1)
                        split_product(da[:, t % 2], 2 * D, [(ht(ht_hi, g, k, s), ht(ht_lo, g, k, s), wa_hi[:, k, :],
                                                             wa_lo[:, k, :]) for k in range(KD)]).then_inc(da_full, 1)
                        pe.wait_ge(p0_ready, b * NT + t)
                        split_product(db, D + 2, [(ht(ht_hi, g, k, s), ht(ht_lo, g, k, s), wb_hi[:, k, :],
                                                   wb_lo[:, k, :]) for k in range(KD)]).then_inc(db_full, 1)

            def layer1_transposes(b, g):
                pe.wait_ge(h1_ready, b * NT + 2 * g + 2)
                transposes(g, lambda g, s: h1[:, g % 2, s, :], tp1_full)

            def layer1_dense(b, g, last):
                pe.wait_ge(ht1_ready, b * NG + g + 1)
                for s in range(2):
                    t = 2 * g + s
                    if t >= 4:
                        pe.wait_ge(y_ready, b * NT + t - 3)
                    elif t == 2:
                        pe.wait_ge(p0_ready, b * NT + (NT if last else 2 * NT))
                    elif t == 3:
                        pe.wait_ge(si_ready, b * NG + (NG if last else 2 * NG))
                    elif not last:
                        pe.wait_ge(g2_ready, b * NT + 2 * NT + t - 1)
                    split_product(l1_bank[t % 4], D, [(ht(ht_hi, g, k, s), ht(ht_lo, g, k, s), wl_hi[:, k, :],
                                                     wl_lo[:, k, :]) for k in range(KD)]).then_inc(l1_full, 1)

            def accumulate(b, i, read, before, ready, n, lhs, rhs):
                s = i % 2
                if i >= 2:
                    pe.wait_ge(read, b * NT + i - 1 + 2 * (read is z_tmp_done))
                elif before is z_tmp_done:
                    pe.wait_ge(before, b * NT + i + 1)
                else:
                    pe.wait_ge(before, b * NT + NT + i - 1)
                for jt in range(NT):
                    if ready is not None and i == 0:
                        pe.wait_ge(ready, b * NT + jt + 1)
                    if lhs is of_a and jt % HJ == 0:
                        pe.wait_ge(a_ready, 2 * (b * NT + NT + i) + jt // HJ + 1)
                    l_hi, l_lo = lhs(i, jt)
                    r_hi, r_lo = rhs(jt)
                    nc.tensor.matmul(acc[:, s, 0:n], l_hi, r_hi, start=(jt == 0), stop=False)
                    nc.tensor.matmul(acc[:, s, 0:D], l_hi, r_lo, start=False, stop=False)
                    ins = nc.tensor.matmul(acc[:, s, 0:n], l_lo, r_hi, start=False, stop=(jt == NT - 1))
                ins.then_inc(acc_full, 1)

            def of_t(i, jt):
                return t_hi[:, i, jt, :], t_lo[:, i, jt, :]

            def of_a(i, jt):
                return a_hi[:, i % 2, jt, :], a_lo[:, i % 2, jt, :]

            def batch(b, last):
                pe.wait_ge(g2_ready, b * NT + NT)
                for i in range(NT):
                    if i % 2 == 0:
                        pe.wait_ge(t_ready, b * NU + i + 2)
                    accumulate(b, i, g1_tmp_ready, z_tmp_done, None, D + 2, of_t, lambda jt: (g2_hi[:, jt, :], g2_lo[:, jt, :]))
                    if i == NT - 2 and not last:
                        layer0_transposes(b + 1, 0)
                if not last:
                    layer0_dense(b + 1)
                for i in range(NT):
                    accumulate(b, i, v_tmp_done, g1_tmp_ready, g1_ready, D, of_t,
                               lambda jt: (g1_hi[:, jt, :], g1_lo[:, jt, :]))
                    if i in (NT - 3, NT - 2):
                        layer1_transposes(b, i - NT + 3)
                for g in range(NG):
                    layer1_dense(b, g, last)
                    if g < 2:
                        layer1_transposes(b, g + 2)
                for i in range(NT):
                    accumulate(b, i, z_tmp_done, v_tmp_done, y_ready, D, of_a, lambda jt: (g1_hi[:, jt, :], g1_lo[:, jt, :]))

            layer0_transposes(0, 0)
            layer0_dense(0)
            with nc.tensor.Fori(0, B - 2, 2) as b:
                batch(b, False)
                batch(b + 1, False)
            batch(B - 2, False)
            batch(B - 1, True)


def kernel(x, adj, L0_gnn_Wv, L0_gnn_bv, L0_gnn_aw, L0_gnn_ab, L0_gnn_Wk, L0_gnn_bk, L1_gnn_kernel, L1_gnn_bias):
    import concourse.bacc as bacc
    from concourse.bass_utils import run_bass_kernel_spmd

    x, adj = np.asarray(x), np.asarray(adj)
    B, N, D = x.shape
    P = 128
    nt = N // P
    adj_t = adj.reshape(B, nt // 2, 2, P, 2, nt // 2, P).transpose(0, 1, 4, 6, 2, 5, 3)
    adj_t = np.ascontiguousarray(adj_t).reshape(B, nt // 2, 2, P, 2, nt // 2 * P)
    arrays = {
        "x": x,
        "adj": adj,
        "adj_t": adj_t,
        "wv_t": np.ascontiguousarray(np.asarray(L0_gnn_Wv).T),
        "bv": np.asarray(L0_gnn_bv),
        "aw": np.asarray(L0_gnn_aw),
        "ab": np.asarray(L0_gnn_ab),
        "wk": np.asarray(L0_gnn_Wk),
        "bk": np.asarray(L0_gnn_bk),
        "w_l1": np.asarray(L1_gnn_kernel),
        "bias_l1": np.asarray(L1_gnn_bias),
    }
    arrays = {f"{k}_dram": np.ascontiguousarray(a) for k, a in arrays.items()}
    nc = bacc.Bacc("TRN2", target_bir_lowering=False, num_devices=1, dynamic_dma_scratch_size=1024)
    args = [nc.dram_tensor(k, a.shape, mybir.dt.from_np(a.dtype), kind="ExternalInput").ap()
            for k, a in arrays.items()]
    out = nc.dram_tensor("out_dram", (B, N, D), F32, kind="ExternalOutput").ap()
    gnn_two_layers(nc, *args, out)
    r = run_bass_kernel_spmd(nc, [arrays], core_ids=[0])
    return r.results[0]["out_dram"]
```

```python
import numpy as np
import concourse.bass as bass
from concourse import mybir
from contextlib import ExitStack

F32 = mybir.dt.float32
F32R = mybir.dt.float32r
ALU = mybir.AluOpType
ACT = mybir.ActivationFunctionType



def gnn_two_layers(nc, x, adj, adj_t, wv_t, bv, aw, ab, wk, bk, w_l1, bias_l1, out):
    B, N, D = x.shape
    P = 128
    NT = N // P
    KD = D // P
    NG = NT // 2
    NU = NT
    HJ = NT // 2
    HALVES = [(k, h) for k in range(NU + 1) for h in range(2)]
    T_D = {2: HALVES[0:1], 3: HALVES[1:2]}
    T_V = {-1: HALVES[2:3], 1: HALVES[3:4], 2: HALVES[4:5], 3: HALVES[5:6], 4: HALVES[6:7]}
    T_Z = {i: HALVES[7 + i:8 + i] for i in range(8)}
    T_U = {i: HALVES[15 + i:16 + i] for i in range(3)}
    BEFORE_U = 15
    ROWS_U = {0: (0,), 1: (1,), 2: (2,), 3: (3, 4), 4: (5, 6), 5: (7,)}
    STATS_V = {0: (0, 1)}
    STATS_U = {0: (2, 3), 1: (4,), 2: (5, 6), 3: (7,)}
    DIAG_Z = {0: 4, 1: 5, 3: 6, 4: 7}
    A_FIRST = {i: (i + 2, 1) for i in (0, 2, 3, 4, 5)} | {1: (4, 0)}
    A_THEN = {0: (3, 1)} | {i: (i + 3, 0) for i in (2, 3, 4)}
    LOW_ON_POOL = (0, 1, 6, 7)
    TS, RS = 2, 4
    PHASES = 3 * NT
    EPS_LN, EPS_ROW, SLOPE = 1e-5, 1e-12, 0.2

    ctx = ExitStack()
    with ctx:
        def sb(name, shape, dt=F32):
            return ctx.enter_context(nc.sbuf_tensor(name, shape, dt))

        def pb(name, shape):
            return ctx.enter_context(nc.psum_tensor(name, shape, F32))

        def sem(name):
            return ctx.enter_context(nc.semaphore(name))

        t_hi = sb("t_hi", [P, NT, NT, P], F32R)
        t_lo = sb("t_lo", [P, NT, NT, P], F32R)
        tg_a = sb("tg_a", [P, TS, 2, HJ, P])
        tg_e = sb("tg_e", [P, TS, 2, HJ, P])
        a_raw = sb("a_raw", [P, RS, N])
        a_hi = sb("a_hi", [P, 2, NT, P], F32R)
        a_lo = sb("a_lo", [P, 2, NT, P], F32R)
        wa_hi = sb("wa_hi", [P, KD, 2 * D], F32R)
        wa_lo = sb("wa_lo", [P, KD, 2 * D], F32R)
        wb_hi = sb("wb_hi", [P, KD, D + 2], F32R)
        wb_lo = sb("wb_lo", [P, KD, D + 2], F32R)
        wl_hi = sb("wl_hi", [P, KD, D], F32R)
        wl_lo = sb("wl_lo", [P, KD, D], F32R)
        vi_hi = sb("vi_hi", [P, KD, P], F32R)
        vi_lo = sb("vi_lo", [P, KD, P], F32R)
        h0 = sb("h0", [P, NT, D])
        h1 = sb("h1", [P, 2, 2, D])
        x_res = sb("x_res", [P, 2, D])
        ht_hi = sb("ht_hi", [P, 2, KD, 2 * P], F32R)
        ht_lo = sb("ht_lo", [P, 2, KD, 2 * P], F32R)
        p0 = sb("p0", [P, 2, NT, D])
        p1 = sb("p1", [P, NT, D])
        g2_hi = sb("g2_hi", [P, NT, D + 2], F32R)
        g2_lo = sb("g2_lo", [P, NT, D], F32R)
        g1_hi = sb("g1_hi", [P, NT, D], F32R)
        g1_lo = sb("g1_lo", [P, NT, D], F32R)
        g1_tmp = sb("g1_tmp", [P, 2, D])
        si = sb("si", [P, N])
        sj = sb("sj", [P, NT])
        z_tmp = sb("z_tmp", [P, 2, D])
        o_tile = sb("o_tile", [P, 2, D])
        bk_sum = sb("bk_sum", [P, D])
        bias1 = sb("bias1", [P, D])
        ident = sb("ident", [P, P])
        st0 = sb("st0", [P, NT, 6])
        st1 = sb("st1", [P, NT, 6])
        mv0 = sb("mv0", [P, NT, 2])
        mv1 = sb("mv1", [P, NT, 2])
        ve0 = sb("ve0", [P, NT])
        ve1 = sb("ve1", [P, NT])
        rstd0 = sb("rstd0", [P, NT])
        rstd1 = sb("rstd1", [P, NT])
        row_a = sb("row_a", [P, NT])
        row_a1 = sb("row_a1", [P, NT])
        dh = sb("dh", [P, NT])
        mhalf = sb("mhalf", [P, NT])
        row_t = sb("row_t", [P, NT])
        rinv = sb("rinv", [P, NT])
        aw_s = sb("aw_s", [P, 2 * KD])
        bv_s = sb("bv_s", [P, KD])
        ab_s = sb("ab_s", [P, 1])
        bv_r = sb("bv_r", [P, KD, P])
        v_s = sb("v_s", [P, KD + 1, 2])
        cst = sb("cst", [P, 2])

        wk_raw = p0[:, 1].rearrange("p (a k) n -> p a k n", k=KD)
        wvt_raw = p1[:, 0:KD, :]
        bk_raw = p0[:, 0, 0:3, :]

        tp = pb("tp", [P, 2, KD, 2 * P])
        da = pb("da", [P, 2, 2 * D])
        db = pb("db", [P, 512])
        ps = pb("ps", [P, 512])
        acc = pb("acc", [P, 2, 512])

        l1_bank = [da[:, 0, :], da[:, 1, :], db[:, :], ps[:, :]]

        loaded_c = sem("loaded_c")
        setup = sem("setup")
        ident_zero = sem("ident_zero")
        ident_ready = sem("ident_ready")
        v_ready = sem("v_ready")
        weights_ready = sem("weights_ready")
        h0_loaded = sem("h0_loaded")
        x_res_loaded = [sem(f"x_res_loaded{s}") for s in range(2)]
        tg_loaded = [sem(f"tg_loaded{s}") for s in range(TS)]
        raw_loaded = [sem(f"raw_loaded{s}") for s in range(RS)]
        stored = [sem(f"stored{s}") for s in range(2)]
        tp0_full, tp1_full = sem("tp0_full"), sem("tp1_full")
        si_full = sem("si_full")
        da_full, db_full, l1_full = sem("da_full"), sem("db_full"), sem("l1_full")
        acc_full = sem("acc_full")
        ht0_hi_done, ht1_hi_done = sem("ht0_hi_done"), sem("ht1_hi_done")
        ht0_ready, ht1_ready = sem("ht0_ready"), sem("ht1_ready")
        si_ready = sem("si_ready")
        g2_hi_done, g2_ready = sem("g2_hi_done"), sem("g2_ready")
        p0_ready = sem("p0_ready")
        score_done, leaky_done, e_ready = sem("score_done"), sem("leaky_done"), sem("e_ready")
        prod_ready = sem("prod_ready")
        t_hi_done, t_ready = sem("t_hi_done"), sem("t_ready")
        row_t_done, rinv_done = sem("row_t_done"), sem("rinv_done")
        g1_tmp_ready, g1_hi_done, g1_ready = sem("g1_tmp_ready"), sem("g1_hi_done"), sem("g1_ready")
        rows_done, rows1_done, dh_ready = sem("rows_done"), sem("rows1_done"), sem("dh_ready")
        stats0, mean0, ve0_ready, rstd0_ready = (sem(n) for n in ("stats0", "mean0", "ve0_ready", "rstd0_ready"))
        stats1, mean1, ve1_ready, rstd1_ready = (sem(n) for n in ("stats1", "mean1", "ve1_ready", "rstd1_ready"))
        weights_rounded = sem("weights_rounded")
        z_half_full = sem("z_half_full")
        slot_seen = sem("slot_seen")
        stats_seen = sem("stats_seen")
        h0_ready, h1_ready = sem("h0_ready"), sem("h1_ready")
        v_tmp_done, x1_ready = sem("v_tmp_done"), sem("x1_ready")
        y_hi_done, y_ready = sem("y_hi_done"), sem("y_ready")
        diag_done = sem("diag_done")
        a_hi_done = [sem(f"a_hi_done{h}") for h in range(2)]
        a_ready = [sem(f"a_ready{h}") for h in range(2)]
        z_tmp_done, o_ready = sem("z_tmp_done"), sem("o_ready")

        x_v = x.rearrange("b (t p) d -> b p t d", p=P)
        out_v = out.rearrange("b (t p) d -> b p t d", p=P)
        adj_v = adj.rearrange("b (t p) j -> b p t j", p=P)

        def chunk(src, b, i):
            return src[b, i // 2, :, :, i % 2].rearrange("h p c -> p h c")

        def t_view(t, u):
            cp, jh = u // 2, u % 2
            return t[:, 2 * cp:2 * cp + 2, jh * HJ:(jh + 1) * HJ, :]

        def a_half(part, i, h):
            return part[:, i % 2, h * HJ:(h + 1) * HJ].rearrange("p q i -> p (q i)")

        def load_t_unit(eng, b, u):
            eng.dma_start(tg_a[:, u % TS].rearrange("p s q i -> p (s q i)"),
                          adj_t[b, u // 2, u % 2].rearrange("p s c -> p (s c)")).then_inc(tg_loaded[u % TS], 16)

        def next_unit(b, u, last):
            if u + TS < NU:
                return b, u + TS
            return None if last else (b + 1, u + TS - NU)

        block = ctx.enter_context(nc.Block())

        @block.sync
        def _(sp):
            sp.dma_start(h0[:, :, :], x_v[0]).then_inc(h0_loaded, 16)
            sp.dma_start(wk_raw[:, 0:3], wk.rearrange("a (k p) n -> p a k n", p=P)).then_inc(loaded_c, 16)
            sp.dma_start(wk_raw[:, 3], w_l1.rearrange("(k p) n -> p k n", p=P)).then_inc(loaded_c, 16)
            sp.dma_start(wvt_raw, wv_t.rearrange("(k p) n -> p k n", p=P)).then_inc(loaded_c, 16)
            sp.dma_start(bk_raw, bk.rearrange("(o a) n -> o a n", o=1).to_broadcast([P, 3, D])).then_inc(loaded_c, 16)
            sp.dma_start(bias1[:, :], bias_l1.rearrange("(o n) -> o n", o=1).to_broadcast([P, D])).then_inc(loaded_c, 16)
            with nc.allow_non_contiguous_dma(reason="three short vectors"):
                sp.dma_start(aw_s[:, :], aw.rearrange("(c p) o -> p (c o)", p=P)).then_inc(loaded_c, 16)
                sp.dma_start(bv_s[:, :], bv.rearrange("(c p) -> p c", p=P)).then_inc(loaded_c, 16)
                sp.dma_start(ab_s[:, :], ab.rearrange("(o n) -> o n", o=1).to_broadcast([P, 1])).then_inc(loaded_c, 16)
            def rows(b, tiles):
                for t in tiles:
                    if t < RS:
                        sp.wait_ge(a_ready[1], b * NT + NT - RS + t + 1)
                    else:
                        sp.wait_ge(rows_done, b * NT + t - RS + 1)
                    sp.dma_start(a_raw[:, t % RS, :], adj_v[b, :, t]).then_inc(raw_loaded[t % RS], 16)

            def stores(b, i):
                sp.wait_ge(o_ready, b * NT + i + 1)
                sp.dma_start(out_v[b, :, i], o_tile[:, i % 2, :]).then_inc(stored[i % 2], 16)

            def load_chunk(b, i):
                if i < RS:
                    sp.wait_ge(rows_done, b * NT + NT - RS + i + 1)
                else:
                    sp.wait_ge(a_ready[1], b * NT + i - RS + 1 + NT)
                sp.sem_inc(slot_seen, 1)
                sp.dma_start(a_raw[:, i % RS, :].rearrange("p (h c) -> p h c", h=2),
                             chunk(adj_t, b, i)).then_inc(raw_loaded[i % RS], 16)

            def load_h0(b):
                sp.wait_ge(tp0_full, b * NG)
                sp.dma_start(h0[:, :, :], x_v[b]).then_inc(h0_loaded, 16)

            def batch(b, left):
                rows(b, range(RS, NT))
                for i in range(RS):
                    load_chunk(b, i)
                if left > 1:
                    load_h0(b + 2)
                for i in range(NT):
                    sp.wait_ge(x1_ready, b * NT + i + 1)
                    sp.dma_start(x_res[:, i % 2, :], x_v[b, :, i]).then_inc(x_res_loaded[i % 2], 16)
                    if i in (RS, RS + 1):
                        load_chunk(b, i)
                for i in range(RS, NT):
                    if i >= RS + 2:
                        load_chunk(b, i)
                    stores(b, i - RS)
                for i in range(NT - RS, NT):
                    if left > 0:
                        rows(b + 1, (i - NT + RS,))
                    stores(b, i)

            load_h0(1)
            rows(0, range(RS))
            with nc.sync.Fori(0, B - 3, 2) as b:
                batch(b, 2)
                batch(b + 1, 2)
            batch(B - 2, 1)
            batch(B - 1, 0)
            for s in range(2):
                sp.wait_ge(stored[s], 16 * (B * NT // 2 + 1))

        @block.gpsimd
        def _(pool):
            pool.sem_inc(a_ready[0], NT)
            pool.sem_inc(a_ready[1], NT)
            nc.gpsimd.memset(mhalf[:, :], -0.5)
            nc.gpsimd.memset(ident[:, :], 0.0).then_inc(ident_zero, 1)
            pool.wait_ge(ident_zero, 1)
            nc.gpsimd.affine_select(out=ident[:, :], in_=ident[:, :], compare_op=ALU.not_equal, fill=1.0,
                                    base=0, pattern=[[-1, P]], channel_multiplier=1).then_inc(ident_ready, 1)

            def power(dst, src, ready, count, done, c=slice(0, NT)):
                pool.wait_ge(ready, count)
                nc.gpsimd.tensor_tensor(dst[:, c], src[:, c], mhalf[:, c], ALU.pow).then_inc(done, 1)

            def g1_split(b, i):
                pool.wait_ge(g1_hi_done, b * NT + i + 1)
                nc.gpsimd.tensor_tensor(g1_lo[:, i, :], g1_tmp[:, i % 2, :], g1_hi[:, i, :].bitcast(F32),
                                        ALU.subtract).then_inc(g1_ready, 1)

            def a_split(b, i, h):
                pool.wait_ge(a_hi_done[h], b * NT + i + 1)
                nc.gpsimd.tensor_tensor(a_half(a_lo, i, h), a_raw[:, i % RS, h * N // 2:(h + 1) * N // 2],
                                        a_half(a_hi, i, h).bitcast(F32), ALU.subtract).then_inc(a_ready[h], 1)

            def t_low(b, u):
                pool.wait_ge(t_hi_done, b * NU + u + 1)
                nc.gpsimd.tensor_tensor(t_view(t_lo, u), tg_e[:, u % TS], t_view(t_hi, u).bitcast(F32),
                                        ALU.subtract).then_inc(t_ready, 1)

            def batch(b, last):
                for i in range(NT):
                    g1_split(b, i)
                    for k, half in T_U.get(i, ()):
                        if half == 1 and k - 1 in LOW_ON_POOL:
                            t_low(b, k - 1)
                    if i == 3 and not last:
                        power(rstd0, ve0, ve0_ready, b + 2, rstd0_ready)
                power(dh, row_a1, rows1_done, b + 1, dh_ready)
                for i, h in ((0, 0), (0, 1), (1, 0), (1, 1)):
                    a_split(b, i, h)
                for i in range(-1, NT):
                    if i % 2 and i > 0:
                        g = i // 2
                        power(rstd1, ve1, ve1_ready, b * NG + g + 1, rstd1_ready, slice(2 * g, 2 * g + 2))
                    for k, half in T_V.get(i, ()):
                        if half == 1 and k - 1 in LOW_ON_POOL and not last:
                            t_low(b + 1, k - 1)
                a_split(b, 2, 0)
                a_split(b, 3, 0)
                for i in range(NT):
                    for halves in (A_FIRST, A_THEN):
                        if i in halves:
                            a_split(b, *halves[i])
                    for k, half in T_Z.get(i, ()):
                        if half == 1 and k - 1 in LOW_ON_POOL and not last:
                            t_low(b + 1, k - 1)

            power(rstd0, ve0, ve0_ready, 1, rstd0_ready)
            for k, half in HALVES[:BEFORE_U]:
                if half == 1 and k - 1 in LOW_ON_POOL:
                    t_low(0, k - 1)
            with nc.gpsimd.Fori(0, B - 3, 2) as b:
                batch(b, False)
                batch(b + 1, False)
            batch(B - 2, False)
            batch(B - 1, True)

        @block.scalar
        def _(act):
            def transposed_hi(g, full, b, done):
                act.wait_ge(full, b * NG + g + 1)
                nc.scalar.activation(ht_hi[:, g % 2], tp[:, g % 2], ACT.Relu).then_inc(done, 1)

            def dense0(b, t):
                act.wait_ge(da_full, b * NT + t + 1)
                nc.scalar.copy(p1[:, t, :], da[:, t % 2, 0:D])
                nc.scalar.copy(g2_hi[:, t, 0:D], da[:, t % 2, D:2 * D]).then_inc(g2_hi_done, 1)

            def si_copy(b, g):
                act.wait_ge(si_full, b * NG + g + 1)
                nc.scalar.copy(si[:, g * 2 * P:(g + 1) * 2 * P], ps[:, 0:2 * P]).then_inc(si_ready, 1)

            def t_step(b, k, half, last, first=False, between=None):
                s = k % TS
                if half == 0 and k < NU:
                    if not (first and k < TS):
                        act.wait_ge(t_ready, b * NU + k - TS + 1)
                    c = slice(k // 2 * 2 * P, (k // 2 + 1) * 2 * P)
                    for q in range(HJ):
                        jt = k % 2 * HJ + q
                        if q == HJ // 2 and between is not None:
                            between()
                        ins = nc.scalar.activation(tg_e[:, s, :, q, :], si[:, c].rearrange("p (s i) -> p s i", s=2),
                                                   ACT.Identity, bias=sj[:, jt:jt + 1])
                    ins.then_inc(score_done, 1)
                if half == 1 and k > 0:
                    u = k - 1
                    if not first:
                        act.wait_ge(acc_full, (b - 1) * PHASES + NT + 2 * (u // 2) + 2)
                    act.wait_ge(prod_ready, b * NU + u + 1)
                    nc.scalar.copy(t_view(t_hi, u), tg_e[:, u % TS]).then_inc(t_hi_done, 1)
                    nxt = next_unit(b, u, last)
                    if nxt is not None:
                        load_t_unit(act, *nxt)
                if half == 1 and between is not None:
                    between()
                if half == 1 and k < NU:
                    act.wait_ge(leaky_done, b * NU + k + 1)
                    nc.scalar.activation(tg_e[:, s], tg_e[:, s], ACT.Exp).then_inc(e_ready, 1)

            def layer0_dense(b, between=lambda g: None):
                for g in range(NG):
                    if g + 1 < NG:
                        transposed_hi(g + 1, tp0_full, b, ht0_hi_done)
                    si_copy(b, g)
                    dense0(b, 2 * g)
                    dense0(b, 2 * g + 1)
                    between(g)

            def rows(b, t):
                act.wait_ge(raw_loaded[t % RS], 16 * (b * (2 * NT // RS) + t // RS + 1))
                nc.scalar.activation(a_raw[:, t % RS, :], a_raw[:, t % RS, :], ACT.Copy,
                                     accum_out=row_a[:, t:t + 1]).then_inc(rows_done, 1)

            def l1_scaled(b, t):
                act.wait_ge(l1_full, b * NT + t + 1)
                nc.scalar.activation(g1_hi[:, t, :], l1_bank[t % 4][:, 0:D], ACT.Copy,
                                     scale=dh[:, t:t + 1]).then_inc(y_hi_done, 1)

            def a_round(b, i, h):
                if h == 0:
                    act.wait_ge(diag_done, b * NT + i + 1)
                if i >= 2 and h == 0:
                    act.wait_ge(z_half_full, b * NT + i - 1)
                elif i >= 2:
                    act.wait_ge(acc_full, b * PHASES + 2 * NT + i - 1)
                nc.scalar.copy(a_half(a_hi, i, h), a_raw[:, i % RS, h * N // 2:(h + 1) * N // 2]).then_inc(a_hi_done[h], 1)

            def batch(b, last):
                for i in range(NT):
                    if i == NT - 1 and not last:
                        transposed_hi(0, tp0_full, b + 1, ht0_hi_done)
                    act.wait_ge(g1_tmp_ready, b * NT + i + 1)
                    nc.scalar.copy(g1_hi[:, i, :], g1_tmp[:, i % 2, :]).then_inc(g1_hi_done, 1)
                    for step in T_U.get(i, ()):
                        t_step(b, *step, last, first=True)
                    for t in ROWS_U.get(i, ()):
                        rows(b, t)
                def between(g):
                    if g == NG - 1:
                        a_round(b, 0, 0)
                        a_round(b, 0, 1)
                    if not last:
                        for step in T_D.get(g, ()):
                            t_step(b + 1, *step, False)

                if not last:
                    layer0_dense(b + 1, between)
                else:
                    between(NG - 1)
                for i in range(-1, NT):
                    if not last:
                        for step in T_V.get(i, ()):
                            t_step(b + 1, *step, False)
                    if i == 0:
                        a_round(b, 1, 0)
                        a_round(b, 1, 1)
                    if i == 6:
                        transposed_hi(0, tp1_full, b, ht1_hi_done)
                    if i == 7:
                        transposed_hi(1, tp1_full, b, ht1_hi_done)
                act.wait_ge(dh_ready, b + 1)
                for g in range(NG):
                    if g == NG - 1:
                        a_round(b, 2, 0)
                        a_round(b, 3, 0)
                    if g in (0, 2):
                        l1_scaled(b, 2 * g)
                        transposed_hi(g // 2 + 2, tp1_full, b, ht1_hi_done)
                    else:
                        l1_scaled(b, 2 * g)
                    l1_scaled(b, 2 * g + 1)
                for i in range(NT):
                    if i in A_FIRST:
                        a_round(b, *A_FIRST[i])

                    def next_half():
                        if i in A_THEN:
                            a_round(b, *A_THEN[i])
                    if not last:
                        (step,) = T_Z[i]
                        t_step(b + 1, *step, False, between=next_half)
                    else:
                        next_half()

            transposed_hi(0, tp0_full, 0, ht0_hi_done)
            act.wait_ge(loaded_c, 16 * 8)
            load_t_unit(act, 0, 0)
            load_t_unit(act, 0, 1)
            for a in range(2):
                nc.scalar.copy(wa_hi[:, :, a * D:(a + 1) * D], wk_raw[:, a + 1])
            nc.scalar.copy(wb_hi[:, :, 0:D], wk_raw[:, 0])
            nc.scalar.copy(wl_hi[:, :, :], wk_raw[:, 3]).then_inc(weights_rounded, 1)

            def first_steps(g):
                for step in T_D.get(g, ()):
                    t_step(0, *step, False, first=True)

            layer0_dense(0, first_steps)
            for step in HALVES[2:BEFORE_U]:
                t_step(0, *step, False, first=True)
            with nc.scalar.Fori(0, B - 3, 2) as b:
                batch(b, False)
                batch(b + 1, False)
            batch(B - 2, False)
            batch(B - 1, True)

        @block.vector
        def _(dve):
            dve.sem_inc(z_tmp_done, 2)
            for s in range(2):
                dve.sem_inc(stored[s], 16)
            dve.sem_inc(x1_ready, 2)
            steps = [0]

            def then(ins):
                steps[0] += 1
                ins.then_inc(setup, 1)
                dve.wait_ge(setup, steps[0])

            def moments(count, st, mv, ve, stats, mean, ve_ready, tiles):
                dve.wait_ge(stats, count)
                dve.sem_inc(stats_seen, 1)
                for t in tiles:
                    ins = nc.vector.bn_aggr(mv[:, t, :], st[:, t, :])
                ins.then_inc(mean, 1)
                dve.wait_ge(mean, count)
                c = slice(tiles[0], tiles[-1] + 1)
                nc.vector.tensor_scalar_add(ve[:, c], mv[:, c, 1], EPS_LN).then_inc(ve_ready, 1)

            def stats0_of(t):
                ins = nc.vector.bn_stats(st0[:, t, :], h0[:, t, :])
                if t == NT - 1:
                    ins.then_inc(stats0, 1)

            def moments0(count):
                moments(count, st0, mv0, ve0, stats0, mean0, ve0_ready, range(NT))

            def norm(dst, src, t, mv, rstd, ready):
                nc.vector.tensor_scalar(dst, src, mv[:, t, 0:1], rstd[:, t:t + 1],
                                        ALU.subtract, ALU.mult).then_inc(ready, 1)

            def norm0(g):
                for t in (2 * g, 2 * g + 1):
                    norm(h0[:, t, :], h0[:, t, :], t, mv0, rstd0, h0_ready)

            def norm1(b, par, g):
                dve.wait_ge(rstd1_ready, b * NG + g + 1)
                if g >= 2:
                    dve.wait_ge(tp1_full, b * NG + g - 1)
                for s in range(2):
                    norm(h1[:, g % 2, s, :], p0[:, par, 2 * g + s, :], 2 * g + s, mv1, rstd1, h1_ready)

            def transposed_lo(g, hi_done, b, ready):
                dve.wait_ge(hi_done, b * NG + g + 1)
                nc.vector.scalar_tensor_tensor(out=ht_lo[:, g % 2], in0=tp[:, g % 2], scalar=0.0,
                                               in1=ht_hi[:, g % 2].bitcast(F32),
                                               op0=ALU.max, op1=ALU.subtract).then_inc(ready, 1)

            def dense0(b, par, t):
                dve.wait_ge(g2_hi_done, b * NT + t + 1)
                nc.vector.tensor_tensor(g2_lo[:, t, :], da[:, t % 2, D:2 * D], g2_hi[:, t, 0:D].bitcast(F32),
                                        ALU.subtract).then_inc(g2_ready, 1)
                dve.wait_ge(db_full, b * NT + t + 1)
                nc.vector.tensor_tensor(p0[:, par, t, :], db[:, 0:D], bk_sum[:, :], ALU.add)
                nc.vector.tensor_tensor(sj[:, t:t + 1], db[:, D:D + 1], cst[:, 1:2], ALU.add).then_inc(p0_ready, 1)

            def layer0_dense(b, par, between=lambda g: None):
                for g in range(NG):
                    if g + 1 < NG:
                        transposed_lo(g + 1, ht0_hi_done, b, ht0_ready)
                    if g + 2 < NG:
                        norm0(g + 2)
                    dense0(b, par, 2 * g)
                    dense0(b, par, 2 * g + 1)
                    between(g)

            def t_step(b, k, half):
                u, s = k - 1, (k - 1) % TS
                if half == 0 and k > 0:
                    dve.wait_ge(e_ready, b * NU + u + 1)
                    dve.wait_ge(tg_loaded[s], 16 * (b * (NU // TS) + u // TS + 1))
                    nc.vector.tensor_tensor(tg_e[:, s], tg_a[:, s], tg_e[:, s], ALU.mult).then_inc(prod_ready, 1)
                if half == 1 and k < NU:
                    dve.wait_ge(score_done, b * NU + k + 1)
                    e = tg_e[:, k % TS]
                    nc.vector.scalar_tensor_tensor(out=e, in0=e, scalar=SLOPE, in1=e,
                                                   op0=ALU.mult, op1=ALU.max).then_inc(leaky_done, 1)
                if half == 1 and k > 0 and u not in LOW_ON_POOL:
                    dve.wait_ge(t_hi_done, b * NU + u + 1)
                    nc.vector.tensor_tensor(t_view(t_lo, u), tg_e[:, s], t_view(t_hi, u).bitcast(F32),
                                            ALU.subtract).then_inc(t_ready, 1)

            def u_chunk(b, i):
                s = i % 2
                dve.wait_ge(acc_full, b * PHASES + i + 1)
                nc.vector.tensor_scalar_add(row_t[:, i:i + 1], acc[:, s, D:D + 1], EPS_ROW).then_inc(row_t_done, 1)
                dve.wait_ge(row_t_done, b * NT + i + 1)
                nc.vector.reciprocal(rinv[:, i:i + 1], row_t[:, i:i + 1]).then_inc(rinv_done, 1)
                dve.wait_ge(rinv_done, b * NT + i + 1)
                if i >= 2:
                    dve.wait_ge(g1_ready, b * NT + i - 1)
                nc.vector.scalar_tensor_tensor(out=g1_tmp[:, s, :], in0=acc[:, s, 0:D], scalar=rinv[:, i:i + 1],
                                               in1=p1[:, i, :], op0=ALU.mult, op1=ALU.add).then_inc(g1_tmp_ready, 1)

            def v_chunk(b, par, i):
                s, x1 = i % 2, p0[:, par, i, :]
                dve.wait_ge(acc_full, b * PHASES + NT + i + 1)
                nc.vector.scalar_tensor_tensor(out=x1, in0=acc[:, s, 0:D], scalar=rinv[:, i:i + 1],
                                               in1=x1, op0=ALU.mult, op1=ALU.add).then_inc(v_tmp_done, 1)
                dve.wait_ge(v_tmp_done, b * NT + i + 1)
                dve.wait_ge(x_res_loaded[s], 16 * (b * (NT // 2) + i // 2 + 1))
                nc.vector.scalar_tensor_tensor(out=x1, in0=x1, scalar=0.0, in1=x_res[:, s, :],
                                               op0=ALU.max, op1=ALU.add).then_inc(x1_ready, 1)
                if i == NT - 1:
                    transposed_lo(2, ht1_hi_done, b, ht1_ready)
                dve.wait_ge(x1_ready, b * NT + i + 3)
                ins = nc.vector.bn_stats(st1[:, i, :], x1)
                if i % 2:
                    ins.then_inc(stats1, 1)

            def diag(b, i):
                dve.wait_ge(raw_loaded[i % RS], 16 * (b * (2 * NT // RS) + NT // RS + i // RS + 1))
                blk = a_raw[:, i % RS, i * P:(i + 1) * P]
                nc.vector.tensor_tensor(blk, blk, ident[:, :], ALU.add).then_inc(diag_done, 1)

            def l1_low(b, t):
                dve.wait_ge(y_hi_done, b * NT + t + 1)
                nc.vector.scalar_tensor_tensor(out=g1_lo[:, t, :], in0=l1_bank[t % 4][:, 0:D], scalar=dh[:, t:t + 1],
                                               in1=g1_hi[:, t, :].bitcast(F32), op0=ALU.mult, op1=ALU.subtract)\
                    .then_inc(y_ready, 1)

            def z_chunk(b, par, i):
                s = i % 2
                dve.wait_ge(acc_full, b * PHASES + 2 * NT + i + 1)
                nc.vector.scalar_tensor_tensor(out=z_tmp[:, s, :], in0=acc[:, s, 0:D], scalar=dh[:, i:i + 1],
                                               in1=bias1[:, :], op0=ALU.mult, op1=ALU.add).then_inc(z_tmp_done, 1)
                dve.wait_ge(z_tmp_done, b * NT + i + 3)
                dve.wait_ge(stored[s], 16 * (b * (NT // 2) + i // 2 + 1))
                nc.vector.scalar_tensor_tensor(out=o_tile[:, s, :], in0=z_tmp[:, s, :], scalar=0.0,
                                               in1=p0[:, par, i, :], op0=ALU.max, op1=ALU.add).then_inc(o_ready, 1)

            def batch(b, par, left):
                last = left == 0
                for i in range(NT):
                    if i == NT - 1 and not last:
                        transposed_lo(0, ht0_hi_done, b + 1, ht0_ready)
                    u_chunk(b, i)
                    for step in T_U.get(i, ()):
                        t_step(b, *step)
                    if not last:
                        for t in STATS_U.get(i, ()):
                            stats0_of(t)
                        if i == 3:
                            moments0(b + 2)
                        if i == NT - 3:
                            dve.wait_ge(rstd0_ready, b + 2)
                            norm0(0)
                            norm0(1)
                def between(g):
                    if g == 0:
                        dve.wait_ge(rows_done, b * NT + NT)
                        nc.vector.tensor_scalar_add(row_a1[:, :], row_a[:, :], 1.0).then_inc(rows1_done, 1)
                    else:
                        diag(b, g - 1)
                    if not last:
                        for step in T_D.get(g, ()):
                            t_step(b + 1, *step)

                if not last:
                    layer0_dense(b + 1, 1 - par, between)
                else:
                    for g in range(NG):
                        between(g)
                diag(b, 3)
                if not last:
                    for step in T_V[-1]:
                        t_step(b + 1, *step)
                for i in range(NT):
                    if i == 6:
                        transposed_lo(0, ht1_hi_done, b, ht1_ready)
                    v_chunk(b, par, i)
                    if i == NT - 1:
                        l1_low(b, 0)
                    if i % 2:
                        moments(b * NG + i // 2 + 1, st1, mv1, ve1, stats1, mean1, ve1_ready, (i - 1, i))
                    elif i > 0:
                        norm1(b, par, i // 2 - 1)
                    if i == 6:
                        transposed_lo(1, ht1_hi_done, b, ht1_ready)
                    if not last:
                        for step in T_V.get(i, ()):
                            t_step(b + 1, *step)
                    if left > 1:
                        if i == 0:
                            dve.wait_ge(h0_loaded, 16 * (b + 3))
                        for t in STATS_V.get(i, ()):
                            stats0_of(t)
                l1_low(b, 1)
                l1_low(b, 2)
                norm1(b, par, NG - 1)
                l1_low(b, 3)
                l1_low(b, 4)
                transposed_lo(3, ht1_hi_done, b, ht1_ready)
                for t in range(5, NT):
                    l1_low(b, t)
                for i in range(NT):
                    z_chunk(b, par, i)
                    if i in DIAG_Z:
                        diag(b, DIAG_Z[i])
                    if not last:
                        for step in T_Z[i]:
                            t_step(b + 1, *step)

            dve.wait_ge(h0_loaded, 16)
            for t in range(NT):
                stats0_of(t)
            moments0(1)
            dve.wait_ge(rstd0_ready, 1)
            norm0(0)
            norm0(1)

            transposed_lo(0, ht0_hi_done, 0, ht0_ready)

            dve.wait_ge(loaded_c, 16 * 8)
            nc.vector.memset(g2_hi[:, :, D:D + 2].bitcast(F32), 1.0)
            nc.vector.memset(wb_hi[:, :, D + 1:D + 2].bitcast(F32), 0.0)
            nc.vector.memset(wb_lo[:, :, D + 1:D + 2].bitcast(F32), 0.0)
            nc.vector.tensor_tensor(bk_sum[:, :], bk_raw[:, 0, :], bk_raw[:, 1, :], ALU.add)
            for k in range(KD):
                ins = nc.vector.tensor_copy(bv_r[:, k, :], bv_s[:, k:k + 1].to_broadcast([P, P]))
            then(ins)
            nc.vector.tensor_tensor(bk_sum[:, :], bk_sum[:, :], bk_raw[:, 2, :], ALU.add)
            dve.wait_ge(weights_rounded, 1)
            for a in range(2):
                nc.vector.tensor_tensor(wa_lo[:, :, a * D:(a + 1) * D], wk_raw[:, a + 1],
                                        wa_hi[:, :, a * D:(a + 1) * D].bitcast(F32), ALU.subtract)
            nc.vector.tensor_tensor(wb_lo[:, :, 0:D], wk_raw[:, 0], wb_hi[:, :, 0:D].bitcast(F32), ALU.subtract)
            nc.vector.tensor_tensor(wl_lo[:, :, :], wk_raw[:, 3], wl_hi[:, :, :].bitcast(F32),
                                    ALU.subtract).then_inc(weights_ready, 1)
            dve.wait_ge(v_ready, 1)
            then(nc.vector.tensor_copy(v_s[:, :, :], db[:, 0:2 * (KD + 1)].rearrange("p (k c) -> p k c", c=2)))
            nc.vector.tensor_tensor(cst[:, 0:1], v_s[:, KD, 0:1], v_s[:, KD, 1:2], ALU.add)
            nc.vector.tensor_copy(wb_hi[:, :, D:D + 1], v_s[:, 0:KD, 0:1])
            for k in range(KD):
                ins = nc.vector.tensor_copy(vi_hi[:, k, :], v_s[:, k, 1:2].to_broadcast([P, P]))
            then(ins)
            nc.vector.tensor_tensor(cst[:, 1:2], cst[:, 0:1], ab_s[:, :], ALU.add)
            nc.vector.tensor_tensor(wb_lo[:, :, D:D + 1], v_s[:, 0:KD, 0:1], wb_hi[:, :, D:D + 1].bitcast(F32),
                                    ALU.subtract)
            for k in range(KD):
                ins = nc.vector.tensor_tensor(vi_lo[:, k, :], v_s[:, k, 1:2].to_broadcast([P, P]),
                                              vi_hi[:, k, :].bitcast(F32), ALU.subtract)
            ins.then_inc(weights_ready, 1)

            def first_steps(g):
                for step in T_D.get(g, ()):
                    t_step(0, *step)

            layer0_dense(0, 0, first_steps)
            for step in HALVES[2:BEFORE_U]:
                t_step(0, *step)
            dve.wait_ge(h0_loaded, 32)
            for tiles in STATS_V.values():
                for t in tiles:
                    stats0_of(t)
            with nc.vector.Fori(0, B - 3, 2) as b:
                batch(b, 0, 2)
                batch(b + 1, 1, 2)
            batch(B - 2, 0, 1)
            batch(B - 1, 1, 0)

        @block.tensor
        def _(pe):
            def transposes(g, tile, full):
                for s in range(2):
                    for k in range(KD):
                        ins = nc.tensor.transpose(tp[:, g % 2, k, s * P:(s + 1) * P],
                                                  tile(g, s)[:, k * P:(k + 1) * P], ident[:, :])
                ins.then_inc(full, 1)

            def split_product(dst, n, pairs):
                for c, (l_hi, l_lo, r_hi, r_lo) in enumerate(pairs):
                    for a, (l, r) in enumerate(((l_hi, r_hi), (l_hi, r_lo), (l_lo, r_hi))):
                        ins = nc.tensor.matmul(dst[:, 0:n], l, r, start=(c == 0 and a == 0),
                                               stop=(c == len(pairs) - 1 and a == 2))
                return ins

            def ht(part, g, k, s):
                return part[:, g % 2, k, s * P:(s + 1) * P]

            def layer0_transposes(b, g):
                pe.wait_ge(h0_ready, b * NT + 2 * g + 2)
                transposes(g, lambda g, s: h0[:, 2 * g + s, :], tp0_full)

            def layer0_dense(b):
                for g in range(NG):
                    if g + 1 < NG:
                        layer0_transposes(b, g + 1)
                    pe.wait_ge(ht0_ready, b * NG + g + 1)
                    pe.wait_ge(si_ready, b * NG + g)
                    split_product(ps, 2 * P, [(vi_hi[:, k, :], vi_lo[:, k, :], ht_hi[:, g % 2, k, :],
                                               ht_lo[:, g % 2, k, :]) for k in range(KD)]).then_inc(si_full, 1)
                    for s in range(2):
                        t = 2 * g + s
                        if t >= 2:
                            pe.wait_ge(g2_ready, b * NT + t - 1)
                        split_product(da[:, t % 2], 2 * D, [(ht(ht_hi, g, k, s), ht(ht_lo, g, k, s), wa_hi[:, k, :],
                                                             wa_lo[:, k, :]) for k in range(KD)]).then_inc(da_full, 1)
                        pe.wait_ge(p0_ready, b * NT + t)
                        split_product(db, D + 2, [(ht(ht_hi, g, k, s), ht(ht_lo, g, k, s), wb_hi[:, k, :],
                                                   wb_lo[:, k, :]) for k in range(KD)]).then_inc(db_full, 1)

            def layer1_transposes(b, g):
                pe.wait_ge(h1_ready, b * NT + 2 * g + 2)
                transposes(g, lambda g, s: h1[:, g % 2, s, :], tp1_full)

            def layer1_dense(b, g, last):
                pe.wait_ge(ht1_ready, b * NG + g + 1)
                for s in range(2):
                    t = 2 * g + s
                    if t >= 4:
                        pe.wait_ge(y_ready, b * NT + t - 3)
                    elif t == 2:
                        pe.wait_ge(p0_ready, b * NT + (NT if last else 2 * NT))
                    elif t == 3:
                        pe.wait_ge(si_ready, b * NG + (NG if last else 2 * NG))
                    elif not last:
                        pe.wait_ge(g2_ready, b * NT + 2 * NT + t - 1)
                    split_product(l1_bank[t % 4], D, [(ht(ht_hi, g, k, s), ht(ht_lo, g, k, s), wl_hi[:, k, :],
                                                     wl_lo[:, k, :]) for k in range(KD)]).then_inc(l1_full, 1)

            def accumulate(b, i, read, before, ready, n, lhs, rhs, tiles=range(NT)):
                s = i % 2
                if tiles[0] > 0:
                    pass
                elif i >= 2:
                    pe.wait_ge(read, b * NT + i - 1 + 2 * (read is z_tmp_done))
                elif before is z_tmp_done:
                    pe.wait_ge(before, b * NT + i + 1)
                else:
                    pe.wait_ge(before, b * NT + NT + i - 1)
                for jt in tiles:
                    if ready is not None and i == 0:
                        pe.wait_ge(ready, b * NT + jt + 1)
                    if lhs is of_a and jt % HJ == 0:
                        pe.wait_ge(a_ready[jt // HJ], b * NT + NT + i + 1)
                    l_hi, l_lo = lhs(i, jt)
                    r_hi, r_lo = rhs(jt)
                    nc.tensor.matmul(acc[:, s, 0:n], l_hi, r_hi, start=(jt == 0), stop=False)
                    nc.tensor.matmul(acc[:, s, 0:D], l_hi, r_lo, start=False, stop=False)
                    ins = nc.tensor.matmul(acc[:, s, 0:n], l_lo, r_hi, start=False, stop=(jt == NT - 1))
                    if lhs is of_a and jt == HJ - 1:
                        ins.then_inc(z_half_full, 1)
                if tiles[-1] == NT - 1:
                    ins.then_inc(acc_full, 1)

            def of_t(i, jt):
                return t_hi[:, i, jt, :], t_lo[:, i, jt, :]

            def of_a(i, jt):
                return a_hi[:, i % 2, jt, :], a_lo[:, i % 2, jt, :]

            def batch(b, last):
                pe.wait_ge(g2_ready, b * NT + NT)
                for i in range(NT):
                    if i % 2 == 0:
                        pe.wait_ge(t_ready, b * NU + i + 2)
                    accumulate(b, i, g1_tmp_ready, z_tmp_done, None, D + 2, of_t, lambda jt: (g2_hi[:, jt, :], g2_lo[:, jt, :]))
                    if i == NT - 2 and not last:
                        layer0_transposes(b + 1, 0)
                if not last:
                    layer0_dense(b + 1)
                for i in range(NT):
                    accumulate(b, i, v_tmp_done, g1_tmp_ready, g1_ready, D, of_t,
                               lambda jt: (g1_hi[:, jt, :], g1_lo[:, jt, :]))
                    if i in (NT - 3, NT - 2):
                        layer1_transposes(b, i - NT + 3)
                def z_chunk(i, tiles=range(NT)):
                    accumulate(b, i, z_tmp_done, v_tmp_done, y_ready, D, of_a,
                               lambda jt: (g1_hi[:, jt, :], g1_lo[:, jt, :]), tiles)

                layer1_dense(b, 0, last)
                layer1_transposes(b, 2)
                layer1_dense(b, 1, last)
                layer1_dense(b, 2, last)
                layer1_transposes(b, 3)
                z_chunk(0, range(HJ))
                z_chunk(1, range(HJ))
                layer1_dense(b, 3, last)
                z_chunk(0, range(HJ, NT))
                z_chunk(1, range(HJ, NT))
                for i in range(2, NT):
                    z_chunk(i)

            pe.wait_ge(ident_ready, 1)
            layer0_transposes(0, 0)
            pe.wait_ge(loaded_c, 16 * 8)
            pe.wait_ge(setup, 1)
            aw_v = aw_s[:, :].rearrange("p (c k) -> p k c", k=KD)
            for m in range(KD + 1):
                for k in range(KD):
                    w = wvt_raw[:, k, m * P:(m + 1) * P] if m < KD else bv_r[:, k, :]
                    ins = nc.tensor.matmul(db[:, 2 * m:2 * m + 2], w, aw_v[:, k, :], start=(k == 0), stop=(k == KD - 1))
            ins.then_inc(v_ready, 1)
            pe.wait_ge(weights_ready, 2)
            layer0_dense(0)
            with nc.tensor.Fori(0, B - 3, 2) as b:
                batch(b, False)
                batch(b + 1, False)
            batch(B - 2, False)
            batch(B - 1, True)


def kernel(x, adj, L0_gnn_Wv, L0_gnn_bv, L0_gnn_aw, L0_gnn_ab, L0_gnn_Wk, L0_gnn_bk, L1_gnn_kernel, L1_gnn_bias):
    import concourse.bacc as bacc
    from concourse.bass_utils import run_bass_kernel_spmd

    x, adj = np.asarray(x), np.asarray(adj)
    B, N, D = x.shape
    P = 128
    nt = N // P
    adj_t = adj.reshape(B, nt // 2, 2, P, 2, nt // 2, P).transpose(0, 1, 4, 6, 2, 5, 3)
    adj_t = np.ascontiguousarray(adj_t).reshape(B, nt // 2, 2, P, 2, nt // 2 * P)
    arrays = {
        "x": x,
        "adj": adj,
        "adj_t": adj_t,
        "wv_t": np.ascontiguousarray(np.asarray(L0_gnn_Wv).T),
        "bv": np.asarray(L0_gnn_bv),
        "aw": np.asarray(L0_gnn_aw),
        "ab": np.asarray(L0_gnn_ab),
        "wk": np.asarray(L0_gnn_Wk),
        "bk": np.asarray(L0_gnn_bk),
        "w_l1": np.asarray(L1_gnn_kernel),
        "bias_l1": np.asarray(L1_gnn_bias),
    }
    arrays = {f"{k}_dram": np.ascontiguousarray(a) for k, a in arrays.items()}
    nc = bacc.Bacc("TRN2", target_bir_lowering=False, num_devices=1, dynamic_dma_scratch_size=1024)
    args = [nc.dram_tensor(k, a.shape, mybir.dt.from_np(a.dtype), kind="ExternalInput").ap()
            for k, a in arrays.items()]
    out = nc.dram_tensor("out_dram", (B, N, D), F32, kind="ExternalOutput").ap()
    gnn_two_layers(nc, *args, out)
    r = run_bass_kernel_spmd(nc, [arrays], core_ids=[0])
    return r.results[0]["out_dram"]
```
